# Optimizing a Trainium2 kernel written in Bass

```python
import numpy as np
import jax
import jax.numpy as jnp

def _softmax(x, axis=-1):
    return jax.nn.softmax(x, axis=axis)

def _gelu(x):
    return jax.nn.gelu(x, approximate=True)

def _silu(x):
    return jax.nn.silu(x)

def _sigmoid(x):
    return jax.nn.sigmoid(x)

def _layernorm(x, axis=-1, eps=1e-05):
    m = jnp.mean(x, axis=axis, keepdims=True)
    v = jnp.var(x, axis=axis, keepdims=True)
    return (x - m) / jnp.sqrt(v + eps)

def _scatter_add(tgt, idx, src, axis=0):
    return tgt.at[idx].add(src)

def _segment_sum(src, seg, n):
    return jax.ops.segment_sum(src, seg, n)
kernel_name = 'mk_cond_seq_d2_seqx_r4_2e5cb8'

def setup_inputs(seed: int=0):
    np.random.seed(seed)
    _w = jnp.asarray

    def _rec_inputs():
        import jax
        import jax.numpy as jnp
        _rk = jax.random.key(seed)
        x = 7.22e-05 + 1 * jax.random.normal(jax.random.fold_in(_rk, 1), (2, 1024, 256), jnp.float32)
        _lenS = 1024 - jax.random.randint(jax.random.fold_in(_rk, 7), (2,), 0, max(1, 1024 // 4) + 1, jnp.int32)
        _lenS2 = 1024 - jax.random.randint(jax.random.fold_in(_rk, 8), (2,), 0, max(1, 1024 // 4) + 1, jnp.int32)
        cond_2048 = 0.00386106 + 1.00199 * jax.random.normal(jax.random.fold_in(_rk, 11), (2, 512), jnp.float32)
        _validS = jnp.arange(1024)[None, :] < _lenS[:, None]
        _validS2 = jnp.arange(1024)[None, :] < _lenS2[:, None]
        _causal = jnp.tril(jnp.ones((1024, 1024), dtype=bool))
        mask_BxS_ff1 = jnp.where(jnp.ones((2, 1024), dtype=bool), 1.0, 0.0).astype(jnp.float32)
        mask_BxSx1_fk1 = jnp.where(jnp.ones((2, 1024, 1), dtype=bool), 1.0, 0.0).astype(jnp.float32)
        return (x, cond_2048, mask_BxS_ff1, mask_BxSx1_fk1)
    x, cond_2048, mask_BxS_ff1, mask_BxSx1_fk1 = _rec_inputs()

    def _L0_cond_setup():
        import jax, jax.numpy as jnp
        import numpy as np
        B, T, D, H, TE = (8, 256, 256, 16, 512)
        LN_EPS = 1e-05

        def layer_norm(x, w, b):
            m = jnp.mean(x, axis=-1, keepdims=True)
            v = jnp.var(x, axis=-1, keepdims=True)
            return (x - m) / jnp.sqrt(v + LN_EPS) * w + b
        key = jax.random.key(seed)
        ks = jax.random.split(key, 8)
        s = lambda k, sh: jax.random.normal(k, sh, jnp.float32) * 0.02
        return dict(x=jax.random.normal(ks[0], (B, T, D), jnp.float32), emb=jax.random.normal(ks[1], (B, TE), jnp.float32), src_mask=jnp.ones((B, T), jnp.float32), norm_w=jnp.ones((D,), jnp.float32), norm_b=jnp.zeros((D,), jnp.float32), q_w=s(ks[2], (D, D)), q_b=jnp.zeros((D,), jnp.float32), k_w=s(ks[3], (D, D)), k_b=jnp.zeros((D,), jnp.float32), v_w=s(ks[4], (D, D)), v_b=jnp.zeros((D,), jnp.float32), emb_w=s(ks[5], (TE, 2 * D)), emb_b=jnp.zeros((2 * D,), jnp.float32), sb_norm_w=jnp.ones((D,), jnp.float32), sb_norm_b=jnp.zeros((D,), jnp.float32), out_w=s(ks[6], (D, D)), out_b=jnp.zeros((D,), jnp.float32))
    _L0_cond_all = _L0_cond_setup()
    _L0_cond_in = {k: v for k, v in _L0_cond_all.items() if k in ('norm_w', 'norm_b', 'q_w', 'q_b', 'k_w', 'k_b', 'v_w', 'v_b', 'emb_w', 'emb_b', 'sb_norm_w', 'sb_norm_b', 'out_w', 'out_b')}
    del _L0_cond_all

    def _L1_cond_setup():
        import jax, jax.numpy as jnp
        import numpy as np
        B, T, D, H, TE = (4, 512, 256, 8, 512)
        EPS = 1e-05

        def _ln(x, w, b):
            m = jnp.mean(x, axis=-1, keepdims=True)
            v = jnp.mean((x - m) ** 2, axis=-1, keepdims=True)
            return (x - m) * jax.lax.rsqrt(v + EPS) * w + b
        key = jax.random.key(seed)
        ks = jax.random.split(key, 16)
        s = 0.02
        inp = {'x': jax.random.normal(ks[0], (B, T, D), jnp.float32), 'emb': jax.random.normal(ks[1], (B, TE), jnp.float32), 'src_mask': (jax.random.uniform(ks[2], (B, T, 1)) > 0.2).astype(jnp.float32), 'num_head': H, 'ln_w': jnp.ones((D,), jnp.float32), 'ln_b': jnp.zeros((D,), jnp.float32), 'Wq': jax.random.normal(ks[3], (D, D), jnp.float32) * s, 'bq': jnp.zeros((D,), jnp.float32), 'Wk': jax.random.normal(ks[4], (D, D), jnp.float32) * s, 'bk': jnp.zeros((D,), jnp.float32), 'Wv': jax.random.normal(ks[5], (D, D), jnp.float32) * s, 'bv': jnp.zeros((D,), jnp.float32), 'W_emb': jax.random.normal(ks[6], (TE, 2 * D), jnp.float32) * s, 'b_emb': jnp.zeros((2 * D,), jnp.float32), 'ln2_w': jnp.ones((D,), jnp.float32), 'ln2_b': jnp.zeros((D,), jnp.float32), 'W_out': jax.random.normal(ks[7], (D, D), jnp.float32) * s, 'b_out': jnp.zeros((D,), jnp.float32)}
        return inp
    _L1_cond_all = _L1_cond_setup()
    _L1_cond_in = {k: v for k, v in _L1_cond_all.items() if k in ('ln_w', 'ln_b', 'Wq', 'bq', 'Wk', 'bk', 'Wv', 'bv', 'W_emb', 'b_emb', 'ln2_w', 'ln2_b', 'W_out', 'b_out')}
    del _L1_cond_all
    return {'x': x, 'cond_2048': cond_2048, 'mask_BxS_ff1': mask_BxS_ff1, 'mask_BxSx1_fk1': mask_BxSx1_fk1, 'L0_cond_norm_w': _L0_cond_in['norm_w'], 'L0_cond_norm_b': _L0_cond_in['norm_b'], 'L0_cond_q_w': _L0_cond_in['q_w'], 'L0_cond_q_b': _L0_cond_in['q_b'], 'L0_cond_k_w': _L0_cond_in['k_w'], 'L0_cond_k_b': _L0_cond_in['k_b'], 'L0_cond_v_w': _L0_cond_in['v_w'], 'L0_cond_v_b': _L0_cond_in['v_b'], 'L0_cond_emb_w': _L0_cond_in['emb_w'], 'L0_cond_emb_b': _L0_cond_in['emb_b'], 'L0_cond_sb_norm_w': _L0_cond_in['sb_norm_w'], 'L0_cond_sb_norm_b': _L0_cond_in['sb_norm_b'], 'L0_cond_out_w': _L0_cond_in['out_w'], 'L0_cond_out_b': _L0_cond_in['out_b'], 'L1_cond_ln_w': _L1_cond_in['ln_w'], 'L1_cond_ln_b': _L1_cond_in['ln_b'], 'L1_cond_Wq': _L1_cond_in['Wq'], 'L1_cond_bq': _L1_cond_in['bq'], 'L1_cond_Wk': _L1_cond_in['Wk'], 'L1_cond_bk': _L1_cond_in['bk'], 'L1_cond_Wv': _L1_cond_in['Wv'], 'L1_cond_bv': _L1_cond_in['bv'], 'L1_cond_W_emb': _L1_cond_in['W_emb'], 'L1_cond_b_emb': _L1_cond_in['b_emb'], 'L1_cond_ln2_w': _L1_cond_in['ln2_w'], 'L1_cond_ln2_b': _L1_cond_in['ln2_b'], 'L1_cond_W_out': _L1_cond_in['W_out'], 'L1_cond_b_out': _L1_cond_in['b_out']}

def reference(x, cond_2048, mask_BxS_ff1, mask_BxSx1_fk1, L0_cond_norm_w, L0_cond_norm_b, L0_cond_q_w, L0_cond_q_b, L0_cond_k_w, L0_cond_k_b, L0_cond_v_w, L0_cond_v_b, L0_cond_emb_w, L0_cond_emb_b, L0_cond_sb_norm_w, L0_cond_sb_norm_b, L0_cond_out_w, L0_cond_out_b, L1_cond_ln_w, L1_cond_ln_b, L1_cond_Wq, L1_cond_bq, L1_cond_Wk, L1_cond_bk, L1_cond_Wv, L1_cond_bv, L1_cond_W_emb, L1_cond_b_emb, L1_cond_ln2_w, L1_cond_ln2_b, L1_cond_W_out, L1_cond_b_out):
    import jax
    import jax.numpy as jnp

    def _L0_cond_ref(x, emb, src_mask, norm_w, norm_b, q_w, q_b, k_w, k_b, v_w, v_b, emb_w, emb_b, sb_norm_w, sb_norm_b, out_w, out_b):
        import jax, jax.numpy as jnp
        import numpy as np
        B, T, D, H, TE = (8, 256, 256, 16, 512)
        LN_EPS = 1e-05

        def layer_norm(x, w, b):
            m = jnp.mean(x, axis=-1, keepdims=True)
            v = jnp.var(x, axis=-1, keepdims=True)
            return (x - m) / jnp.sqrt(v + LN_EPS) * w + b
        Bx, Tx, Dx = x.shape
        xn = layer_norm(x, norm_w, norm_b)
        q = (xn @ q_w + q_b).reshape(Bx, Tx, H, -1)
        k = (xn @ k_w + k_b).reshape(Bx, Tx, H, -1)
        att = jnp.einsum('bnhl,bmhl->bnmh', q, k)
        mask = src_mask.reshape(Bx, 1, Tx, 1)
        att = att + (1.0 - mask) * -1000000.0
        att = jax.nn.softmax(att, axis=2)
        v = ((xn @ v_w + v_b) * src_mask[:, :, None]).reshape(Bx, Tx, H, -1)
        y = jnp.einsum('bnmh,bmhl->bnhl', att, v).reshape(Bx, Tx, Dx)
        e = jax.nn.silu(emb) @ emb_w + emb_b
        scale, shift = jnp.split(e[:, None, :], 2, axis=2)
        h = layer_norm(y, sb_norm_w, sb_norm_b) * (1.0 + scale) + shift
        h = jax.nn.silu(h) @ out_w + out_b
        return x + h

    def _L1_cond_ref(x, emb, src_mask, num_head, ln_w, ln_b, Wq, bq, Wk, bk, Wv, bv, W_emb, b_emb, ln2_w, ln2_b, W_out, b_out):
        import jax, jax.numpy as jnp
        import numpy as np
        B, T, D, H, TE = (4, 512, 256, 8, 512)
        EPS = 1e-05

        def _ln(x, w, b):
            m = jnp.mean(x, axis=-1, keepdims=True)
            v = jnp.mean((x - m) ** 2, axis=-1, keepdims=True)
            return (x - m) * jax.lax.rsqrt(v + EPS) * w + b
        b, t, d = x.shape
        h = num_head
        dh = d // h
        xn = _ln(x, ln_w, ln_b)
        q = xn @ Wq + bq
        k = xn @ Wk + bk + (1.0 - src_mask) * -1000000.0
        q = jax.nn.softmax(q.reshape(b, t, h, dh), axis=-1)
        k = jax.nn.softmax(k.reshape(b, t, h, dh), axis=1)
        v = ((xn @ Wv + bv) * src_mask).reshape(b, t, h, dh)
        att = jnp.einsum('bnhd,bnhl->bhdl', k, v)
        y = jnp.einsum('bnhd,bhdl->bnhl', q, att).reshape(b, t, d)
        emb_out = (jax.nn.silu(emb) @ W_emb + b_emb)[:, None, :]
        scale, shift = jnp.split(emb_out, 2, axis=2)
        hh = _ln(y, ln2_w, ln2_b) * (1.0 + scale) + shift
        hh = jax.nn.silu(hh) @ W_out + b_out
        return x + hh
    x = _L0_cond_ref(x, cond_2048, mask_BxS_ff1, L0_cond_norm_w, L0_cond_norm_b, L0_cond_q_w, L0_cond_q_b, L0_cond_k_w, L0_cond_k_b, L0_cond_v_w, L0_cond_v_b, L0_cond_emb_w, L0_cond_emb_b, L0_cond_sb_norm_w, L0_cond_sb_norm_b, L0_cond_out_w, L0_cond_out_b)
    x = _L1_cond_ref(x, cond_2048, mask_BxSx1_fk1, 8, L1_cond_ln_w, L1_cond_ln_b, L1_cond_Wq, L1_cond_bq, L1_cond_Wk, L1_cond_bk, L1_cond_Wv, L1_cond_bv, L1_cond_W_emb, L1_cond_b_emb, L1_cond_ln2_w, L1_cond_ln2_b, L1_cond_W_out, L1_cond_b_out)
    return x

_drawn_inputs = setup_inputs


def setup_inputs(seed=0):
    import zlib

    import numpy as np

    out = dict(_drawn_inputs(seed))
    spreads = {'L0_cond_norm_w': (1.0, 0.6),
     'L0_cond_norm_b': (0.0, 0.1),
     'L0_cond_q_b': (0.0, 0.8),
     'L0_cond_k_b': (0.0, 0.8),
     'L0_cond_v_b': (0.0, 0.1),
     'L0_cond_emb_b': (0.0, 0.1),
     'L0_cond_sb_norm_w': (1.0, 0.2),
     'L0_cond_sb_norm_b': (0.0, 0.318),
     'L0_cond_out_b': (0.0, 0.1),
     'L1_cond_ln_w': (1.0, 0.6),
     'L1_cond_ln_b': (0.0, 0.1),
     'L1_cond_bq': (0.0, 0.8),
     'L1_cond_bk': (0.0, 0.8),
     'L1_cond_bv': (0.0, 0.1),
     'L1_cond_b_emb': (0.0, 0.299),
     'L1_cond_ln2_w': (1.0, 0.2),
     'L1_cond_ln2_b': (0.0, 0.368),
     'L1_cond_b_out': (0.0, 0.1)}
    factors = {'L0_cond_q_w': 2.978, 'L0_cond_k_w': 2.732, 'L1_cond_Wq': 8.0, 'L1_cond_Wk': 8.0}
    for name, (base, spread) in spreads.items():
        noise = np.random.default_rng([zlib.crc32(name.encode()), seed]).standard_normal(out[name].shape)
        drawn = base * np.exp(spread * noise) if base else spread * noise
        out[name] = jnp.asarray(drawn.astype(out[name].dtype))
    for name, factor in factors.items():
        out[name] = (out[name] * factor).astype(out[name].dtype)
    return out
```

```python
from contextlib import ExitStack

import numpy as np
import concourse.bass as bass
from concourse import mybir


def two_layer_conditioned_attention(
    nc: bass.Bass,
    x, cond, mask0, mask1,
    norm_w, norm_b, q_w, q_b, k_w, k_b, v_w, v_b, emb_w, emb_b, sb_norm_w, sb_norm_b, out_w, out_b,
    ln_w, ln_b, Wq, bq, Wk, bk, Wv, bv, W_emb, b_emb, ln2_w, ln2_b, W_out, b_out,
    out,
):
    F32, BF16 = mybir.dt.float32, mybir.dt.bfloat16
    ALU, ACT, AX = mybir.AluOpType, mybir.ActivationFunctionType, mybir.AxisListType

    B, T, D = x.shape
    P = 128
    NT = T // P
    KC = D // P
    HALF = 512
    NH = T // HALF
    H0, H1 = 16, 8
    DH0, DH1 = D // H0, D // H1
    GH = 4
    GC = GH * DH0
    HG = H0 // GH
    G = B * HG
    E = cond.shape[1]
    EC = E // P
    EPS = 1e-5
    BIG = 1e6

    Q_PART = [0, 0, 0, 1, 1, 2]
    K_PART = [0, 1, 2, 0, 1, 0]
    PARTS = 3
    ROW_MASK = len(Q_PART) * DH0
    ROW_MAX = ROW_MASK + PARTS
    ROWS = ROW_MAX + PARTS
    SLOTS = 3

    UNITS = GH * NT
    MAXES = UNITS * NH
    PER_STEP = 10

    names = ["norm_w", "norm_b", "qk_b", "sb_w", "sb_b", "emb_b0", "ln_w", "ln_b", "bk", "ln2_w", "ln2_b", "emb_b1", "cond", "mask0", "mask1"]
    sizes = [KC, KC, HG, KC, KC, 2 * KC, KC, KC, KC, KC, KC, 2 * KC, B * EC, B * NT, B * NT]
    COL = dict(zip(names, np.concatenate([[0], np.cumsum(sizes)[:-1]]).astype(int).tolist()))
    NV = sum(sizes)

    LN_STEPS = 2 * NT + 1
    LN_BANKS = (NT // 4) * KC
    RING = 4
    UNITS_A = HG * NH + NT
    UNITS_CD = NT + KC * NH + NT + NT + NT // 2 + KC * NH + KC + NT + NT

    ctx = ExitStack()
    with ctx:
        def sb(name, shape, dt=F32):
            return ctx.enter_context(nc.sbuf_tensor(name, shape, dt))

        def sem(name):
            return ctx.enter_context(nc.semaphore(name))

        xs = sb("xs", [P, B * NT, D])
        work = sb("work", [P, 8192])
        parts = sb("parts", [P, G, PARTS, T], BF16)
        qs = sb("qs", [P, SLOTS, GH, T], BF16)
        ks = sb("ks", [P, SLOTS, GH, T], BF16)
        v_all = sb("v_all", [P, G, NT, GC])
        vs = sb("vs", [P, NT, GH, 32])
        y_all = sb("y_all", [P, G, NT, GC])
        yT = sb("yT", [P, T])
        bias_rows = sb("bias_rows", [P, 5, D])
        wo0 = sb("wo0", [P, KC, D])
        ident = sb("ident", [P, P])
        blocks = sb("blocks", [P, P])
        vecs = sb("vecs", [NV, P])
        cols = sb("cols", [P, NV])
        mrow = sb("mrow", [B * NT, P])
        mrest = sb("mrest", [B * NT, 2, P])
        mparts = sb("mparts", [B * NT, PARTS, P], BF16)
        stats = sb("stats", [P, NT, 6])
        mv = sb("mv", [P, NT, 2])
        var = sb("var", [P, NT])
        std = sb("std", [P, NT])
        rstd = sb("rstd", [P, NT])
        halfmax = sb("halfmax", [P, UNITS, NH])
        negmax = sb("negmax", [P, UNITS])
        crest = sb("crest", [UNITS, 2, P])
        cparts = sb("cparts", [UNITS, PARTS, P], BF16)
        rden = sb("rden", [P, NH, 4 * GH, 1])
        scond = sb("scond", [P, B, EC])
        emb = sb("emb", [P, 2, 2 * KC, B])
        modA = sb("modA", [P, 2, B, KC])
        modB = sb("modB", [P, 2, B, KC])
        modS = sb("modS", [P, 2, 2, KC])
        fence = sb("fence", [P, 1])
        kmax = sb("kmax", [P, KC])
        ksum = sb("ksum", [P, KC])
        rksum = sb("rksum", [P, KC])
        qmax = sb("qmax", [P, NT, H1, 1])
        qsum = sb("qsum", [P, NT, H1, 1])
        rqsum = sb("rqsum", [P, NT, H1, 1])
        att = sb("att", [P, KC, P])

        zs = work[:, 0:2048].rearrange("p (t d) -> p t d", d=D)
        hT = work[:, 2048:4096].rearrange("p (k n) -> p k n", k=KC)
        rest = work[:, 4096:5120].rearrange("p (u n) -> p u n", n=HALF)
        rest2 = work[:, 5120:6144].rearrange("p (u n) -> p u n", n=HALF)
        vtmp = work[:, 6144:6656].rearrange("p (u d) -> p u d", d=D)
        prob = work[:, :].rearrange("p (u j n) -> p u j n", u=2, j=GH)
        early = y_all[:, 0:3].rearrange("p g t c -> p (g t c)")
        wqk = early[:, 0:KC * HG * P].rearrange("p (k g c) -> p k g c", k=KC, g=HG)
        wv0 = early[:, 1024:1024 + KC * D].rearrange("p (k c) -> p k c", k=KC)
        late = parts[:, :].rearrange("p g r n -> p (g r n)").bitcast(F32)
        w1 = late[:, 0:2048].rearrange("p (w k c) -> p w k c", w=4, k=KC)
        embw = late[:, 2048:6144].rearrange("p (l e c) -> p l e c", l=2, e=EC)
        kE = late[:, 2048:4096].rearrange("p (k n) -> p k n", k=KC)
        kN = late[:, 4096:6144].rearrange("p (t d) -> p t d", d=D)
        v1 = late[:, 6144:8192].rearrange("p (t d) -> p t d", d=D)
        q1 = late[:, 8192:10240].rearrange("p (t d) -> p t d", d=D)
        qT = late[:, 10240:12288].rearrange("p (k n) -> p k n", k=KC)
        mrows1 = ks[:, 2].rearrange("p j n -> p (j n)").bitcast(F32)
        tmp1 = qs[:, 2].rearrange("p j n -> p (j n)").bitcast(F32)[:, 0:D]

        bank = [ctx.enter_context(nc.psum_tensor(f"bank{i}", [P, 2 * HALF], F32)) for i in range(4)]
        B8 = [bank[i // 2][:, (i % 2) * HALF:(i % 2 + 1) * HALF] for i in range(8)]
        sT = bank[0:2]
        sN = B8[4:6]
        acc = bank[3]

        vec_in, x_in, w_in, wo_in, mask_in = sem("vec_in"), sem("x_in"), sem("w_in"), sem("wo_in"), sem("mask_in")
        mask_out, stack_in, cmax_out, cmax_in, late_in, stored = sem("mask_out"), sem("stack_in"), sem("cmax_out"), sem("cmax_in"), sem("late_in"), sem("stored")
        ident_ready, ones_ready, krows_ready, qrows_ready, blocks_ready = sem("ident_ready"), sem("ones_ready"), sem("krows_ready"), sem("qrows_ready"), sem("blocks_ready")
        vecT_ready, cols_ready, msplit_step, mparts_ready = sem("vecT_ready"), sem("cols_ready"), sem("msplit_step"), sem("mparts_ready")
        ln_step, var_ready, std_ready, z_ready = sem("ln_step"), sem("var_ready"), sem("std_ready"), sem("z_ready")
        zT_ready, hT_ready = sem("zT_ready"), sem("hT_ready")
        pj_ready, pj_read = sem("pj_ready"), sem("pj_read")
        part1_ready, part2_ready, part3_ready = sem("part1_ready"), sem("part2_ready"), sem("part3_ready")
        v_ready = sem("v_ready")
        biased = sem("biased")
        sN_ready, max_done = sem("sN_ready"), sem("max_done")
        neg_ready, cT_ready, csplit_step, cparts_ready = sem("neg_ready"), sem("cT_ready"), sem("csplit_step"), sem("cparts_ready")
        sT_ready, exp_done, vs_ready, pv_done = sem("sT_ready"), sem("exp_done"), sem("vs_ready"), sem("pv_done")
        yT_ready, yN_ready, rden_ready, y_done = sem("yT_ready"), sem("yN_ready"), sem("rden_ready"), sem("y_done")
        scond_ready, emb_ready, mod_step, mod_ready, modS_ready, mrows_ready = sem("scond_ready"), sem("emb_ready"), sem("mod_step"), sem("mod_ready"), sem("modS_ready"), sem("mrows_ready")
        kmax_ready, kexp_ready, rk_ready, rq_ready = sem("kmax_ready"), sem("kexp_ready"), sem("rk_ready"), sem("rq_ready")
        v1_ready, q_step, qsub_ready, qexp_ready = sem("v1_ready"), sem("q_step"), sem("qsub_ready"), sem("qexp_ready")

        mask_rows = nc.dram_tensor("mask_rows", [PARTS, B, T], BF16, kind="Internal").ap()
        max_rows = nc.dram_tensor("max_rows", [PARTS, GH, T], BF16, kind="Internal").ap()

        block = ctx.enter_context(nc.Block())

        def tiles(ap):
            return ap.rearrange("b (t p) d -> p (b t) d", p=P)

        def group_channels(y, t):
            return y[:, :, t, :]

        STACKS = 2 * len(Q_PART) * GH + 1

        @block.sync
        def _(sp):
            def rows(name, src, n):
                sp.dma_start(vecs[COL[name]:COL[name] + n, :], src.rearrange("(r p) -> r p", p=P)).then_inc(vec_in, 16)

            for name, src, n in (("norm_w", norm_w, KC), ("norm_b", norm_b, KC), ("sb_w", sb_norm_w, KC), ("sb_b", sb_norm_b, KC),
                                 ("emb_b0", emb_b, 2 * KC), ("ln_w", ln_w, KC), ("ln_b", ln_b, KC), ("bk", bk, KC),
                                 ("ln2_w", ln2_w, KC), ("ln2_b", ln2_b, KC), ("emb_b1", b_emb, 2 * KC)):
                rows(name, src, n)
            for side, src in enumerate((q_b, k_b)):
                sp.dma_start(vecs[COL["qk_b"]:COL["qk_b"] + HG, side * GC:(side + 1) * GC],
                             src.rearrange("(g c) -> g c", c=GC)).then_inc(vec_in, 16)
            rows("cond", cond.rearrange("b e -> (b e)"), B * EC)
            rows("mask0", mask0.rearrange("b t -> (b t)"), B * NT)
            rows("mask1", mask1.rearrange("b t o -> (b t o)"), B * NT)
            sp.dma_start(xs[:, 0:NT, :], tiles(x)[:, 0:NT, :]).then_inc(x_in, 16)
            sp.dma_start(mrow[:, :], mask0.rearrange("b (t p) -> (b t) p", p=P)).then_inc(mask_in, 16)
            for kc in range(KC):
                for side, src in enumerate((q_w, k_w)):
                    sp.dma_start(wqk[:, kc, :, side * GC:(side + 1) * GC],
                                 src[kc * P:(kc + 1) * P, :].rearrange("p (g c) -> p g c", c=GC)).then_inc(w_in, 16)
            sp.dma_start(wv0, v_w.rearrange("(k p) c -> p k c", p=P)).then_inc(w_in, 16)
            for i, src in enumerate((v_b, out_b, bq, bv, b_out)):
                sp.dma_start(bias_rows[:, i, :], src.partition_broadcast(P)).then_inc(w_in, 16)
            sp.wait_ge(x_in, 16)
            sp.dma_start(xs[:, NT:, :], tiles(x)[:, NT:, :]).then_inc(x_in, 16)
            sp.dma_start(wo0[:, :, :], out_w.rearrange("(k p) c -> p k c", p=P)).then_inc(wo_in, 16)
            sp.wait_ge(mparts_ready, 1)
            sp.dma_start(mask_rows.rearrange("r b (t p) -> (b t) r p", p=P), mparts[:, :, :]).then_inc(mask_out, 16)

            def stack(g, slot):
                for side, (dst, order) in enumerate(((qs, Q_PART), (ks, K_PART))):
                    for r, part in enumerate(order):
                        for j in range(GH):
                            c = side * GC + j * DH0
                            sp.dma_start(dst[r * DH0:(r + 1) * DH0, slot, j, :],
                                         parts[c:c + DH0, g, part, :]).then_inc(stack_in, 16)
                sp.dma_start(ks[ROW_MASK:ROW_MAX, slot, :, :],
                             mask_rows[:, g // HG, :].unsqueeze(1).to_broadcast([PARTS, GH, T])).then_inc(stack_in, 16)

            def load_max(g, slot):
                sp.wait_ge(cparts_ready, g + 1)
                sp.dma_start(max_rows.rearrange("r j (t p) -> (j t) r p", p=P), cparts[:, :, :]).then_inc(cmax_out, 16)
                sp.wait_ge(cmax_out, (g + 1) * 16)
                sp.dma_start(qs[ROW_MAX:ROWS, slot, :, :], max_rows).then_inc(cmax_in, 16)

            sp.wait_ge(mask_out, 16)
            sp.wait_ge(krows_ready, 1)
            sp.wait_ge(qrows_ready, 1)
            sp.wait_ge(part3_ready, HG * NH)
            stack(0, 0)
            sp.wait_ge(stack_in, 16 * STACKS)
            stack(1, 1)
            load_max(0, 0)
            sp.wait_ge(part3_ready, G * NH)

            def serve(g, refill):
                if refill:
                    sp.wait_ge(stack_in, (g + 2) * (16 * STACKS))
                    sp.wait_ge(sT_ready, g * UNITS + 4)
                    stack(g + 2, sp.snap((g + 2) % SLOTS))
                load_max(g + 1, sp.snap((g + 1) % SLOTS) if refill else (g + 1) % SLOTS)

            with sp.Fori(0, G - 2) as g:
                serve(g, True)
            sp.wait_ge(stack_in, G * 16 * STACKS)
            for i, src in enumerate((Wq, Wk, Wv, W_out)):
                sp.dma_start(w1[:, i], src.rearrange("(k p) c -> p k c", p=P)).then_inc(late_in, 16)
            for i, src in enumerate((emb_w, W_emb)):
                sp.dma_start(embw[:, i], src.rearrange("(e p) c -> p e c", p=P)).then_inc(late_in, 16)
            sp.wait_ge(sT_ready, (G - 2) * UNITS + 4)
            sp.dma_start(mrows1, mask1.rearrange("b t o -> (b t o)").partition_broadcast(P)).then_inc(late_in, 16)
            serve(G - 2, False)
            with sp.Fori(0, B) as b:
                sp.wait_ge(pj_read, RING + B * UNITS_A + (b + 1) * UNITS_CD)
                sp.dma_start(tiles(out)[:, bass.ds(b * NT, NT), :], xs[:, bass.ds(b * NT, NT), :]).then_inc(stored, 16)
            sp.wait_ge(stored, B * 16)

        @block.gpsimd
        def _(pool):
            pool.memset(ident[:, :], 0.0).then_inc(ident_ready, 1)
            pool.wait_ge(ident_ready, 1)
            pool.affine_select(out=ident[:, :], in_=ident[:, :], compare_op=ALU.not_equal, fill=1.0, base=0,
                               pattern=[[-1, P]], channel_multiplier=1).then_inc(ident_ready, 1)
            pool.wait_ge(ident_ready, 2)
            pool.memset(ks[96:P, :, :, :], 1.0).then_inc(krows_ready, 1)
            pool.wait_ge(krows_ready, 1)
            pool.memset(vs[:, :, :, DH0:32], 1.0).then_inc(ones_ready, 1)
            pool.memset(blocks[:, :], 0.0).then_inc(blocks_ready, 1)
            pool.wait_ge(blocks_ready, 1)
            for j in range(P // DH1):
                pool.wait_ge(blocks_ready, 1 + j)
                pool.memset(blocks[j * DH1:(j + 1) * DH1, j * DH1:(j + 1) * DH1], 1.0).then_inc(blocks_ready, 1)
            pool.wait_ge(blocks_ready, 1 + P // DH1)
            with pool.Fori(0, B) as b:
                for u in range(HG * NH):
                    hg, n = u // NH, u % NH
                    pool.wait_ge(part2_ready, b * (HG * NH) + u + 1)
                    pool.tensor_tensor(parts[:, b * HG + hg, 2, n * HALF:(n + 1) * HALF], rest[:, u % 2, :],
                                       parts[:, b * HG + hg, 1, n * HALF:(n + 1) * HALF], op=ALU.subtract).then_inc(part3_ready, 1)
            pool.wait_ge(w_in, 16 * (2 * KC + 1 + 5))
            pool.wait_ge(z_ready, B * NT)
            for b in range(B):
                pool.tensor_tensor(xs[:, b * NT:(b + 1) * NT, :], xs[:, b * NT:(b + 1) * NT, :],
                                   bias_rows[:, 1:2, :].to_broadcast([P, NT, D]), op=ALU.add).then_inc(biased, 1)

            def stage_values(g):
                if not isinstance(g, int):
                    pool.wait_ge(pv_done, g * NT)
                pool.tensor_copy(vs[:, :, :, 0:DH0], v_all[:, g, :, :].rearrange("p t (j c) -> p t j c", j=GH)).then_inc(vs_ready, 1)

            pool.wait_ge(v_ready, B * NT)
            pool.wait_ge(ones_ready, 1)
            stage_values(0)
            with pool.Fori(1, G) as g:
                stage_values(g)
            with pool.Fori(0, B) as b:
                pool.wait_ge(z_ready, B * NT + b * 3 * NT + 2 * NT)
                xb = xs[:, bass.ds(b * NT, NT), :]
                pool.tensor_tensor(xb, xb, bias_rows[:, 4:5, :].to_broadcast([P, NT, D]), op=ALU.add).then_inc(biased, 1)

        @block.scalar
        def _(act):
            def ln_tail(L, A, Bc, func):
                act.wait_ge(var_ready, L + 1)
                act.activation(std[:, :], var[:, :], ACT.Sqrt).then_inc(std_ready, 1)
                for i in range(LN_BANKS):
                    q, kc = i // KC, i % KC
                    act.wait_ge(zT_ready, L * LN_BANKS + i + 1)
                    act.activation(hT[:, kc, q * HALF:(q + 1) * HALF], B8[i], func, scale=A(kc), bias=Bc(kc)).then_inc(hT_ready, 1)

            def col(name, i):
                return cols[:, COL[name] + i:COL[name] + i + 1]

            act.wait_ge(cols_ready, 1)
            with act.Fori(0, B) as b:
                ln_tail(b, lambda kc: col("norm_w", kc), lambda kc: col("norm_b", kc), ACT.Identity)
                for u in range(HG * NH):
                    hg, n = u // NH, u % NH
                    dst = parts[:, b * HG + hg, :, n * HALF:(n + 1) * HALF]
                    act.wait_ge(pj_ready, b * UNITS_A + u + 1)
                    act.activation(dst[:, 0, :], B8[4 + u % 4], ACT.Identity, bias=col("qk_b", hg)).then_inc(part1_ready, 1)
                    act.wait_ge(pj_read, RING + b * UNITS_A + u + 1)
                    act.activation(dst[:, 1, :], rest[:, u % 2, :], ACT.Copy).then_inc(part2_ready, 1)
                for i in range(NT):
                    act.wait_ge(pj_read, RING + b * UNITS_A + HG * NH + i + 1)
                    act.activation(v_all[:, bass.ds(b * HG, HG), i, :], vtmp[:, i % 2, :].rearrange("p (g c) -> p g c", g=HG), ACT.Copy,
                                   scale=cols[:, bass.ds(COL["mask0"] + i + b * NT, 1)]).then_inc(v_ready, 1)

            def attend(g, first=False):
                for u in range(UNITS):
                    c, j = u // GH, u % GH
                    act.wait_ge(sT_ready, g * UNITS + u + 1)
                    if j == 0 and c >= 2:
                        act.wait_ge(pv_done, g * NT + c - 1)
                    if j == 0 and c < 2 and not first:
                        act.wait_ge(pv_done, (g - 1) * NT + NT - 1 + c)
                    act.activation(prob[:, c % 2, j, :], sT[u % 2][:, :], ACT.Exp).then_inc(exp_done, 1)
                    if u == GH + 1 and not first:
                        finish(g - 1)

            def finish(g):
                act.wait_ge(pv_done, (g + 1) * NT)
                act.activation(yT[:, :], acc[:, :], ACT.Copy).then_inc(yT_ready, 1)

            act.wait_ge(part3_ready, G * NH)
            attend(0, True)
            with act.Fori(1, G) as g:
                attend(g)
            finish(G - 1)

            act.activation(scond[:, :, :], cols[:, COL["cond"]:COL["cond"] + B * EC], ACT.Silu).then_inc(scond_ready, 1)
            act.wait_ge(mod_ready, 2 * KC)
            with act.Fori(0, B) as b:
                L = B + 3 * b
                at = B * UNITS_A + b * UNITS_CD
                act.wait_ge(modS_ready, 2 * b + 2)
                ln_tail(L, lambda kc: modS[:, 0, 0, kc:kc + 1], lambda kc: modS[:, 1, 0, kc:kc + 1], ACT.Silu)
                ln_tail(L + 1, lambda kc: col("ln_w", kc), lambda kc: col("ln_b", kc), ACT.Identity)
                for kc in range(KC):
                    act.wait_ge(kmax_ready, b * KC + kc + 1)
                    act.activation(kE[:, kc, :], kE[:, kc, :], ACT.Exp, bias=kmax[:, kc:kc + 1], accum_out=ksum[:, kc:kc + 1]).then_inc(kexp_ready, 1)
                for i in range(NT):
                    act.wait_ge(pj_read, RING + at + NT + KC * NH + i + 1)
                    act.activation(v1[:, i, :], v1[:, i, :], ACT.Copy, scale=cols[:, bass.ds(COL["mask1"] + i + b * NT, 1)]).then_inc(v1_ready, 1)
                for s in range(2):
                    act.wait_ge(qsub_ready, 2 * b + s + 1)
                    half = q1[:, s * NT // 2:(s + 1) * NT // 2, :]
                    act.activation(half, half, ACT.Exp).then_inc(qexp_ready, 1)
                ln_tail(L + 2, lambda kc: modS[:, 0, 1, kc:kc + 1], lambda kc: modS[:, 1, 1, kc:kc + 1], ACT.Silu)

        @block.tensor
        def _(pe):
            def ln_transposes(L):
                for q in range(NT // 4):
                    for kc in range(KC):
                        if kc == 0:
                            pe.wait_ge(z_ready, L * NT + 4 * q + 4)
                        for t in range(4):
                            last = pe.transpose(B8[q * KC + kc][:, t * P:(t + 1) * P], zs[:, 4 * q + t, kc * P:(kc + 1) * P], ident[:, :])
                        last.then_inc(zT_ready, 1)

            def product(unit, base, pieces, used=False):
                pe.wait_ge(pj_read, base + unit + 1)
                for i, (o, l, r) in enumerate(pieces):
                    last = pe.matmul(o, l, r, start=(i == 0), stop=(i == len(pieces) - 1))
                last.then_inc(pj_ready, 1)
                return last

            def rows_times(w, t, o):
                return [(o[:, 0:D], hT[:, kc, t * P:(t + 1) * P], w[:, kc, :]) for kc in range(KC)]

            pe.wait_ge(vec_in, 16 * 16)
            pe.wait_ge(ident_ready, 2)
            pe.transpose(B8[7][:, 0:NV], vecs[:, :], ident[0:NV, 0:NV]).then_inc(vecT_ready, 1)
            pe.wait_ge(cols_ready, 1)
            pe.wait_ge(w_in, 16 * (2 * KC + 1 + 5))
            with pe.Fori(0, B) as b:
                ln_transposes(b)
                pe.wait_ge(hT_ready, (b + 1) * LN_BANKS)
                for u in range(HG * NH):
                    hg, n = u // NH, u % NH
                    o = B8[4 + u % 4]
                    product(u, b * UNITS_A, [(o, wqk[:, kc, hg, :], hT[:, kc, n * HALF:(n + 1) * HALF]) for kc in range(KC)])
                for i in range(NT):
                    u = HG * NH + i
                    last = product(u, b * UNITS_A, rows_times(wv0, i, B8[4 + u % 4]))

            def maxima(g, slot, lo, hi, free_before=None):
                for m in range(lo, hi):
                    r, n = m // NH, m % NH
                    j, qt = r // NT, r % NT
                    if m >= 2:
                        pe.wait_ge(max_done, g * MAXES + m - 1)
                    pe.matmul(sN[m % 2], qs[0:ROW_MAX, slot, j, qt * P:(qt + 1) * P], ks[0:ROW_MAX, slot, j, n * HALF:(n + 1) * HALF],
                              start=True, stop=True).then_inc(sN_ready, 1)

            def maxima_rows(g):
                pe.wait_ge(neg_ready, g + 1)
                pe.transpose(sN[0][0:UNITS, 0:P], negmax[:, :], ident[:, :]).then_inc(cT_ready, 1)

            def values(g, c, n):
                if n == 0:
                    pe.wait_ge(exp_done, g * UNITS + (c + 1) * GH)
                    if c == 0:
                        pe.wait_ge(vs_ready, g + 1)
                        if not isinstance(g, int) or g > 0:
                            pe.wait_ge(yT_ready, g)
                for j in range(GH):
                    last = pe.matmul(acc[32 * j:32 * j + 32, n * HALF:(n + 1) * HALF], vs[:, c, j, :], prob[:, c % 2, j, n * HALF:(n + 1) * HALF],
                                     start=(c == 0), stop=(c == NT - 1), skip_group_check=True)
                if n == NH - 1:
                    last.then_inc(pv_done, 1)

            def rows_of_y(g):
                pe.wait_ge(yT_ready, g + 1)
                for n in range(NH):
                    for t in range(4):
                        last = pe.transpose(sN[n][:, t * P:(t + 1) * P], yT[:, (4 * n + t) * P:(4 * n + t + 1) * P], ident[:, :])
                    last.then_inc(yN_ready, 1)

            def attend(g, slot, nslot, first=False, last_group=False):
                pe.wait_ge(cmax_in, (g + 1) * 16)
                if not last_group:
                    pe.wait_ge(stack_in, (g + 2) * (16 * STACKS))
                m = 0
                for c in range(NT):
                    for j in range(GH):
                        u = c * GH + j
                        if u >= 2 or not first:
                            pe.wait_ge(exp_done, g * UNITS + u - 1)
                        for n in range(NH):
                            last = pe.matmul(sT[u % 2][:, n * HALF:(n + 1) * HALF], ks[0:ROWS, slot, j, c * P:(c + 1) * P],
                                             qs[0:ROWS, slot, j, n * HALF:(n + 1) * HALF], start=True, stop=True)
                        last.then_inc(sT_ready, 1)
                        if not last_group:
                            if m == 0:
                                pe.wait_ge(cparts_ready, g + 1)
                            take = min(MAXES, m + 2)
                            maxima(g + 1, nslot, m, take)
                            m = take
                        if j % 2 == 1 and (c > 0 or not first):
                            if c > 0:
                                values(g, c - 1, j // 2)
                            else:
                                values(g - 1, NT - 1, j // 2)
                            if not last_group:
                                take = min(MAXES, m + 1)
                                maxima(g + 1, nslot, m, take)
                                m = take
                    if c == 1 and not first:
                        if not last_group:
                            pe.wait_ge(max_done, (g + 1) * MAXES + m)
                        else:
                            pe.wait_ge(cparts_ready, g + 1)
                        rows_of_y(g - 1)
                        if not last_group:
                            pe.wait_ge(y_done, g * NH)
                if not last_group:
                    assert m == MAXES
                    maxima_rows(g + 1)

            pe.wait_ge(pj_read, RING + B * UNITS_A)
            pe.wait_ge(stack_in, 16 * STACKS)
            maxima(0, 0, 0, MAXES)
            maxima_rows(0)
            pe.wait_ge(vs_ready, 1)
            attend(0, 0, 1, first=True)
            with pe.Fori(1, G - 1) as g:
                attend(g, pe.snap(g % SLOTS), pe.snap((g + 1) % SLOTS))
            attend(G - 1, (G - 1) % SLOTS, 0, last_group=True)
            for n in range(NH):
                values(G - 1, NT - 1, n)
            pe.wait_ge(y_done, (G - 1) * NH)
            rows_of_y(G - 1)

            pe.wait_ge(late_in, 16 * 7)
            pe.wait_ge(scond_ready, 1)
            for l in range(2):
                for oc in range(2 * KC):
                    at = (l * 2 * KC + oc) * B
                    for e in range(EC):
                        last = pe.matmul(B8[0][:, at:at + B], embw[:, l, e, oc * P:(oc + 1) * P], scond[:, :, e],
                                         start=(e == 0), stop=(e == EC - 1))
            last.then_inc(emb_ready, 1)
            pe.wait_ge(mod_step, 2 * 2 * KC)
            BASE = B * UNITS_A
            with pe.Fori(0, B) as b:
                L = B + 3 * b
                at = BASE + b * UNITS_CD
                u = 0

                def ring():
                    return B8[4 + u % 4]

                ln_transposes(L)
                pe.wait_ge(hT_ready, (L + 1) * LN_BANKS)
                for t in range(NT):
                    last = product(u, at, rows_times(wo0, t, ring()))
                    u += 1

                ln_transposes(L + 1)
                pe.wait_ge(hT_ready, (L + 2) * LN_BANKS)
                for kc in range(KC):
                    for n in range(NH):
                        product(u, at, [(ring(), w1[:, 1, i, kc * P:(kc + 1) * P], hT[:, i, n * HALF:(n + 1) * HALF]) for i in range(KC)])
                        u += 1
                for t in range(NT):
                    product(u, at, rows_times(w1[:, 2], t, ring()))
                    u += 1
                for t in range(NT):
                    product(u, at, rows_times(w1[:, 0], t, ring()))
                    u += 1
                for s in range(NT // 2):
                    if s == 0:
                        pe.wait_ge(kexp_ready, (b + 1) * KC)
                    pe.wait_ge(pj_read, at + u + 1)
                    for t in range(2):
                        for kc in range(KC):
                            last = pe.transpose(ring()[:, (t * KC + kc) * P:(t * KC + kc + 1) * P],
                                                kE[:, kc, (2 * s + t) * P:(2 * s + t + 1) * P], ident[:, :])
                    last.then_inc(pj_ready, 1)
                    u += 1
                for kc in range(KC):
                    for n in range(NH):
                        pe.wait_ge(qexp_ready, 2 * b + n + 1)
                        pe.wait_ge(pj_read, at + u + 1)
                        for t in range(4):
                            last = pe.transpose(ring()[:, t * P:(t + 1) * P], q1[:, 4 * n + t, kc * P:(kc + 1) * P], ident[:, :])
                        last.then_inc(pj_ready, 1)
                        u += 1
                pe.wait_ge(pj_read, RING + at + u)
                pe.wait_ge(v1_ready, (b + 1) * NT)
                for kc in range(KC):
                    product(u, at, [(ring()[:, 0:P], kN[:, t, kc * P:(kc + 1) * P], v1[:, t, kc * P:(kc + 1) * P]) for t in range(NT)])
                    u += 1
                pe.wait_ge(pj_read, RING + at + u)
                for t in range(NT):
                    pe.wait_ge(pj_read, at + u + 1)
                    for kc in range(KC):
                        last = pe.matmul(ring()[:, kc * P:(kc + 1) * P], qT[:, kc, t * P:(t + 1) * P], att[:, kc, :], start=True, stop=True)
                    last.then_inc(pj_ready, 1)
                    u += 1

                ln_transposes(L + 2)
                pe.wait_ge(hT_ready, (L + 3) * LN_BANKS)
                for t in range(NT):
                    product(u, at, rows_times(w1[:, 3], t, ring()))
                    u += 1
                assert u == UNITS_CD

        @block.vector
        def _(dve):
            def layer_norm(L, src):
                base = L * LN_STEPS
                for t in range(NT):
                    dve.bn_stats(stats[:, t, :], src(t)).then_inc(ln_step, 1)
                dve.wait_ge(ln_step, base + NT)
                dve.memset(fence[:, :], 0.0)
                for t in range(NT):
                    dve.bn_aggr(mv[:, t, :], stats[:, t, :]).then_inc(ln_step, 1)
                dve.wait_ge(ln_step, base + 2 * NT)
                dve.tensor_scalar_add(var[:, :], mv[:, :, 1], EPS).then_inc(var_ready, 1)
                dve.wait_ge(std_ready, L + 1)
                dve.reciprocal(rstd[:, :], std[:, :]).then_inc(ln_step, 1)
                dve.wait_ge(ln_step, base + LN_STEPS)
                for t in range(NT):
                    dst = zs[:, t, :]
                    s = src(t)
                    if len(s.shape) == 3:
                        dst = dst.rearrange("p (g c) -> p g c", g=HG)
                    dve.tensor_scalar(dst, s, mv[:, t, 0:1], rstd[:, t:t + 1], op0=ALU.subtract, op1=ALU.mult).then_inc(z_ready, 1)

            dve.memset(qs[96:P, :, :, :], 1.0).then_inc(qrows_ready, 1)
            dve.memset(negmax[:, 0:1], 0.0).then_inc(pj_read, RING)
            dve.wait_ge(vecT_ready, 1)
            dve.tensor_copy(cols[:, :], B8[7][:, 0:NV]).then_inc(cols_ready, 1)
            dve.wait_ge(mask_in, 16)
            dve.tensor_scalar(mrest[:, 0, :], mrow[:, :], 1.0, BIG, op0=ALU.subtract, op1=ALU.mult).then_inc(msplit_step, 1)
            dve.wait_ge(msplit_step, 1)
            dve.tensor_copy(mparts[:, 0, :], mrest[:, 0, :]).then_inc(msplit_step, 1)
            dve.wait_ge(msplit_step, 2)
            dve.tensor_tensor(mrest[:, 1, :], mrest[:, 0, :], mparts[:, 0, :], op=ALU.subtract).then_inc(msplit_step, 1)
            dve.wait_ge(msplit_step, 3)
            dve.tensor_copy(mparts[:, 1, :], mrest[:, 1, :]).then_inc(msplit_step, 1)
            dve.wait_ge(msplit_step, 4)
            dve.tensor_tensor(mparts[:, 2, :], mrest[:, 1, :], mparts[:, 1, :], op=ALU.subtract).then_inc(mparts_ready, 1)

            dve.wait_ge(w_in, 16 * (2 * KC + 1 + 5))
            with dve.Fori(0, B) as b:
                dve.wait_ge(x_in, (b + 1) * 16)
                layer_norm(b, lambda t: xs[:, bass.ds(b * NT + t, 1), :].rearrange("p o d -> p (o d)"))
                for u in range(HG * NH):
                    hg, n = u // NH, u % NH
                    c = COL["qk_b"] + hg
                    dve.wait_ge(part1_ready, b * (HG * NH) + u + 1)
                    if u >= 2:
                        dve.wait_ge(part3_ready, b * (HG * NH) + u - 1)
                    dve.scalar_tensor_tensor(out=rest[:, u % 2, :], in0=B8[4 + u % 4], scalar=cols[:, c:c + 1],
                                             in1=parts[:, b * HG + hg, 0, n * HALF:(n + 1) * HALF],
                                             op0=ALU.add, op1=ALU.subtract).then_inc(pj_read, 1)
                dve.wait_ge(part3_ready, (b + 1) * (HG * NH))
                for i in range(NT):
                    u = HG * NH + i
                    dve.wait_ge(pj_ready, b * UNITS_A + u + 1)
                    if i >= 2:
                        dve.wait_ge(v_ready, b * NT + i - 1)
                    dve.tensor_tensor(vtmp[:, i % 2, :], B8[4 + u % 4][:, 0:D], bias_rows[:, 0, :], op=ALU.add).then_inc(pj_read, 1)

            def reduce(g, lo, hi):
                for m in range(lo, hi):
                    r, n = m // NH, m % NH
                    dve.wait_ge(sN_ready, g * MAXES + m + 1)
                    dve.tensor_reduce(halfmax[:, r, n:n + 1], sN[m % 2], axis=AX.X, op=ALU.max, negate=True).then_inc(max_done, 1)

            def split_maxima(g):
                dve.wait_ge(max_done, (g + 1) * MAXES)
                dve.tensor_reduce(negmax[:, :], halfmax[:, :, :], axis=AX.X, op=ALU.min).then_inc(neg_ready, 1)
                dve.wait_ge(cT_ready, g + 1)
                if not isinstance(g, int) or g > 0:
                    dve.wait_ge(cmax_in, g * 16)
                base = g * 3
                src = sN[0][0:UNITS, 0:P]
                dve.tensor_copy(cparts[:, 0, :], src).then_inc(csplit_step, 1)
                dve.wait_ge(csplit_step, base + 1)
                dve.tensor_tensor(crest[:, 0, :], src, cparts[:, 0, :], op=ALU.subtract).then_inc(csplit_step, 1)
                dve.wait_ge(csplit_step, base + 2)
                dve.tensor_copy(cparts[:, 1, :], crest[:, 0, :]).then_inc(csplit_step, 1)
                dve.wait_ge(csplit_step, base + 3)
                dve.tensor_tensor(cparts[:, 2, :], crest[:, 0, :], cparts[:, 1, :], op=ALU.subtract).then_inc(cparts_ready, 1)

            def divide(g):
                for n in range(NH):
                    src = sN[n].rearrange("p (u c) -> p u c", c=32)
                    dve.wait_ge(yN_ready, g * NH + n + 1)
                    dve.reciprocal(rden[:, n, :, :], src[:, :, DH0:DH0 + 1]).then_inc(rden_ready, 1)
                    dve.wait_ge(rden_ready, g * NH + n + 1)
                    dve.tensor_tensor(y_all[:, g, 4 * n:4 * n + 4, :].rearrange("p t (j c) -> p (t j) c", c=DH0), src[:, :, 0:DH0],
                                      rden[:, n, :, :].to_broadcast([P, 4 * GH, DH0]), op=ALU.mult).then_inc(y_done, 1)

            reduce(0, 0, MAXES)
            split_maxima(0)
            reduce(1, 0, MAXES)
            split_maxima(1)
            Y_AT = 2 * PER_STEP
            with dve.Fori(1, G - 1) as g:
                reduce(g + 1, 0, Y_AT)
                divide(g - 1)
                reduce(g + 1, Y_AT, MAXES)
                split_maxima(g + 1)
            divide(G - 2)
            divide(G - 1)

            dve.wait_ge(emb_ready, 1)
            bank_emb = B8[0][:, 0:2 * 2 * KC * B].rearrange("p (l o b) -> p l o b", l=2, b=B)
            n = 0
            for l in range(2):
                for oc in range(2 * KC):
                    c = COL[f"emb_b{l}"] + oc
                    dve.tensor_scalar(emb[:, l, oc, :], bank_emb[:, l, oc, :], cols[:, c:c + 1], None, op0=ALU.add).then_inc(mod_step, 1)
                    n += 1
            dve.wait_ge(mod_step, n)
            for l, (w, s) in enumerate((("sb_w", "sb_b"), ("ln2_w", "ln2_b"))):
                for kc in range(KC):
                    cw, cb = COL[w] + kc, COL[s] + kc
                    dve.tensor_scalar(modA[:, l, :, kc], emb[:, l, kc, :], 1.0, cols[:, cw:cw + 1], op0=ALU.add, op1=ALU.mult).then_inc(mod_step, 1)
                    dve.tensor_scalar(modB[:, l, :, kc], emb[:, l, kc, :], 1.0, cols[:, cb:cb + 1], op0=ALU.add, op1=ALU.mult).then_inc(mod_step, 1)
                    n += 2
            dve.wait_ge(mod_step, n)
            for l in range(2):
                for kc in range(KC):
                    dve.tensor_tensor(modB[:, l, :, kc], modB[:, l, :, kc], emb[:, l, KC + kc, :], op=ALU.add).then_inc(mod_ready, 1)
            dve.wait_ge(late_in, 16 * 7)
            dve.tensor_scalar(mrows1, mrows1, 1.0, BIG, op0=ALU.subtract, op1=ALU.mult).then_inc(mrows_ready, 1)
            dve.wait_ge(mrows_ready, 1)
            dve.wait_ge(mod_ready, 2 * KC)
            dve.wait_ge(blocks_ready, 1 + P // DH1)
            dve.wait_ge(biased, B)
            BASE = B * UNITS_A
            QS = 4
            with dve.Fori(0, B) as b:
                L = B + 3 * b
                at = BASE + b * UNITS_CD
                u = 0

                def ring():
                    return B8[4 + u % 4]

                def xt(t):
                    return xs[:, bass.ds(b * NT + t, 1), :].rearrange("p o d -> p (o d)")

                dve.wait_ge(y_done, G * NH)
                yb = y_all[:, bass.ds(b * HG, HG)]
                dve.wait_ge(hT_ready, L * LN_BANKS)
                dve.tensor_copy(modS[:, 0, :, :], modA[:, :, bass.ds(b, 1), :].rearrange("p l o k -> p (l o) k")).then_inc(modS_ready, 1)
                dve.tensor_copy(modS[:, 1, :, :], modB[:, :, bass.ds(b, 1), :].rearrange("p l o k -> p (l o) k")).then_inc(modS_ready, 1)
                layer_norm(L, lambda t: group_channels(yb, t))
                for t in range(NT):
                    dve.wait_ge(pj_ready, at + u + 1)
                    dve.tensor_tensor(xt(t), xt(t), ring()[:, 0:D], op=ALU.add).then_inc(pj_read, 1)
                    u += 1
                dve.wait_ge(pj_read, RING + at + u)
                dve.memset(fence[:, :], 0.0)
                layer_norm(L + 1, xt)
                for kc in range(KC):
                    c = COL["bk"] + kc
                    for n in range(NH):
                        dve.wait_ge(pj_ready, at + u + 1)
                        dve.scalar_tensor_tensor(out=kE[:, kc, n * HALF:(n + 1) * HALF], in0=ring(), scalar=cols[:, c:c + 1],
                                                 in1=mrows1[:, bass.ds(b * T + n * HALF, HALF)], op0=ALU.add, op1=ALU.add).then_inc(pj_read, 1)
                        u += 1
                    dve.wait_ge(pj_read, RING + at + u)
                    dve.tensor_reduce(kmax[:, kc:kc + 1], kE[:, kc, :], axis=AX.X, op=ALU.max, negate=True).then_inc(kmax_ready, 1)
                for t in range(NT):
                    dve.wait_ge(pj_ready, at + u + 1)
                    dve.tensor_tensor(v1[:, t, :], ring()[:, 0:D], bias_rows[:, 3, :], op=ALU.add).then_inc(pj_read, 1)
                    u += 1
                qb = b * 4
                for t in range(NT):
                    dve.wait_ge(pj_ready, at + u + 1)
                    dve.tensor_tensor(q1[:, t, :], ring()[:, 0:D], bias_rows[:, 2, :], op=ALU.add).then_inc(pj_read, 1)
                    u += 1
                dve.wait_ge(pj_read, RING + at + u)
                hb = NT // 2
                for s in range(2):
                    qh = q1[:, s * hb:(s + 1) * hb, :].rearrange("p t (h c) -> p (t h) c", c=DH1)
                    mx = qmax[:, s * hb:(s + 1) * hb].rearrange("p t h o -> p (t h) o")
                    dve.tensor_reduce(mx, qh, axis=AX.X, op=ALU.max).then_inc(q_step, 1)
                    dve.wait_ge(q_step, qb + s + 1)
                    dve.tensor_tensor(qh, qh, mx.to_broadcast([P, hb * H1, DH1]), op=ALU.subtract).then_inc(qsub_ready, 1)
                for s in range(2):
                    qh = q1[:, s * hb:(s + 1) * hb, :].rearrange("p t (h c) -> p (t h) c", c=DH1)
                    sm = qsum[:, s * hb:(s + 1) * hb].rearrange("p t h o -> p (t h) o")
                    dve.wait_ge(qexp_ready, 2 * b + s + 1)
                    dve.tensor_reduce(sm, qh, axis=AX.X, op=ALU.add).then_inc(q_step, 1)
                dve.wait_ge(q_step, qb + 4)
                dve.reciprocal(rqsum[:, :, :, :], qsum[:, :, :, :]).then_inc(rq_ready, 1)
                for s in range(NT // 2):
                    dve.wait_ge(pj_ready, at + u + 1)
                    dve.tensor_copy(kN[:, 2 * s:2 * s + 2, :].rearrange("p t d -> p (t d)"), ring()).then_inc(pj_read, 1)
                    u += 1
                for kc in range(KC):
                    for n in range(NH):
                        dve.wait_ge(pj_ready, at + u + 1)
                        dve.tensor_copy(qT[:, kc, n * HALF:(n + 1) * HALF], ring()).then_inc(pj_read, 1)
                        u += 1
                dve.wait_ge(kexp_ready, (b + 1) * KC)
                dve.reciprocal(rksum[:, :], ksum[:, :]).then_inc(rk_ready, 1)
                dve.wait_ge(rk_ready, b + 1)
                for kc in range(KC):
                    dve.wait_ge(pj_ready, at + u + 1)
                    dve.scalar_tensor_tensor(out=att[:, kc, :], in0=ring()[:, 0:P], scalar=rksum[:, kc:kc + 1], in1=blocks[:, :],
                                             op0=ALU.mult, op1=ALU.mult).then_inc(pj_read, 1)
                    u += 1
                dve.wait_ge(rq_ready, b + 1)
                for t in range(NT):
                    dve.wait_ge(pj_ready, at + u + 1)
                    dve.tensor_tensor(q1[:, t, :].rearrange("p (h c) -> p h c", c=DH1), ring()[:, 0:D].rearrange("p (h c) -> p h c", c=DH1),
                                      rqsum[:, t].to_broadcast([P, H1, DH1]), op=ALU.mult).then_inc(pj_read, 1)
                    u += 1
                dve.wait_ge(pj_read, RING + at + u)
                layer_norm(L + 2, lambda t: q1[:, t, :])
                dve.wait_ge(biased, B + b + 1)
                for t in range(NT):
                    dve.wait_ge(pj_ready, at + u + 1)
                    dve.tensor_tensor(xt(t), xt(t), ring()[:, 0:D], op=ALU.add).then_inc(pj_read, 1)
                    u += 1
                assert u == UNITS_CD


_INS = ["x", "cond_2048", "mask_BxS_ff1", "mask_BxSx1_fk1",
        "L0_cond_norm_w", "L0_cond_norm_b", "L0_cond_q_w", "L0_cond_q_b", "L0_cond_k_w", "L0_cond_k_b", "L0_cond_v_w", "L0_cond_v_b",
        "L0_cond_emb_w", "L0_cond_emb_b", "L0_cond_sb_norm_w", "L0_cond_sb_norm_b", "L0_cond_out_w", "L0_cond_out_b",
        "L1_cond_ln_w", "L1_cond_ln_b", "L1_cond_Wq", "L1_cond_bq", "L1_cond_Wk", "L1_cond_bk", "L1_cond_Wv", "L1_cond_bv",
        "L1_cond_W_emb", "L1_cond_b_emb", "L1_cond_ln2_w", "L1_cond_ln2_b", "L1_cond_W_out", "L1_cond_b_out"]


def kernel(**inputs):
    import concourse.bacc as bacc
    from concourse.bass_utils import run_bass_kernel_spmd

    nc = bacc.Bacc("TRN2", target_bir_lowering=False, num_devices=1)
    arrays, args = {}, []
    for name in _INS:
        a = np.ascontiguousarray(inputs[name])
        arrays[f"in_{name}"] = a
        args.append(nc.dram_tensor(f"in_{name}", a.shape, mybir.dt.from_np(a.dtype), kind="ExternalInput").ap())
    shape = arrays["in_x"].shape
    args.append(nc.dram_tensor("out_x", shape, mybir.dt.float32, kind="ExternalOutput").ap())
    two_layer_conditioned_attention(nc, *args)
    r = run_bass_kernel_spmd(nc, [arrays], core_ids=[0])
    return r.results[0]["out_x"]
```

```python
from contextlib import ExitStack

import numpy as np
import concourse.bass as bass
from concourse import mybir


def two_layer_conditioned_attention(
    nc: bass.Bass,
    x, cond, mask0, mask1,
    norm_w, norm_b, q_w, q_b, k_w, k_b, v_w, v_b, emb_w, emb_b, sb_norm_w, sb_norm_b, out_w, out_b,
    ln_w, ln_b, Wq, bq, Wk, bk, Wv, bv, W_emb, b_emb, ln2_w, ln2_b, W_out, b_out,
    out,
):
    F32, BF16 = mybir.dt.float32, mybir.dt.bfloat16
    ALU, ACT, AX = mybir.AluOpType, mybir.ActivationFunctionType, mybir.AxisListType

    B, T, D = x.shape
    P = 128
    NT = T // P
    KC = D // P
    HALF = 512
    NH = T // HALF
    H0, H1 = 16, 8
    DH0, DH1 = D // H0, D // H1
    GH = 4
    GC = GH * DH0
    HG = H0 // GH
    G = B * HG
    E = cond.shape[1]
    EC = E // P
    EPS = 1e-5
    BIG = 1e6

    Q_PART = [0, 0, 0, 1, 1, 2]
    K_PART = [0, 1, 2, 0, 1, 0]
    PARTS = 3
    ROW_MASK = len(Q_PART) * DH0
    ROW_MAX = ROW_MASK + PARTS
    ROWS = ROW_MAX + PARTS
    SLOTS = 3

    UNITS = GH * NT
    MAXES = UNITS * NH

    names = ["norm_w", "norm_b", "qk_b", "sb_w", "sb_b", "emb_b0", "ln_w", "ln_b", "bk", "ln2_w", "ln2_b", "emb_b1", "cond", "mask0", "mask1"]
    sizes = [KC, KC, HG, KC, KC, 2 * KC, KC, KC, KC, KC, KC, 2 * KC, B * EC, B * NT, B * NT]
    COL = dict(zip(names, np.concatenate([[0], np.cumsum(sizes)[:-1]]).astype(int).tolist()))
    NV = sum(sizes)

    LN_STEPS = 2 * NT + 1
    LN_BANKS = (NT // 4) * KC
    RING = 4
    UNITS_A = HG * NH + NT
    UNITS_CD = NT + KC * NH + NT + NT + NT // 2 + KC * NH + KC + NT + NT

    ctx = ExitStack()
    with ctx:
        def sb(name, shape, dt=F32):
            return ctx.enter_context(nc.sbuf_tensor(name, shape, dt))

        def sem(name):
            return ctx.enter_context(nc.semaphore(name))

        xs = sb("xs", [P, B * NT, D])
        work = sb("work", [P, 8192])
        parts = sb("parts", [P, G, PARTS, T], BF16)
        qs = sb("qs", [P, SLOTS, GH, T], BF16)
        ks = sb("ks", [P, SLOTS, GH, T], BF16)
        v_all = sb("v_all", [P, G, NT, GC])
        vs = sb("vs", [P, NT, GH, 32])
        y_all = sb("y_all", [P, G, NT, GC])
        yT = sb("yT", [P, T])
        bias_rows = sb("bias_rows", [P, 5, D])
        wo0 = sb("wo0", [P, KC, D])
        ident = sb("ident", [P, P])
        blocks = sb("blocks", [P, P])
        vecs = sb("vecs", [NV, P])
        cols = sb("cols", [P, NV])
        mrow = sb("mrow", [B * NT, P])
        mrest = sb("mrest", [B * NT, 2, P])
        mparts = sb("mparts", [B * NT, PARTS, P], BF16)
        stats = sb("stats", [P, NT, 6])
        mv = sb("mv", [P, NT, 2])
        var = sb("var", [P, NT])
        std = sb("std", [P, NT])
        rstd = sb("rstd", [P, NT])
        halfmax = sb("halfmax", [P, UNITS, NH])
        negmax = sb("negmax", [P, UNITS])
        crest = sb("crest", [UNITS, 1, P])
        cparts = sb("cparts", [UNITS, PARTS, P], BF16)
        rden = sb("rden", [P, NH, 4 * GH, 1])
        scond = sb("scond", [P, B, EC])
        emb = sb("emb", [P, 2, 2 * KC, B])
        modA = sb("modA", [P, 2, B, KC])
        modB = sb("modB", [P, 2, B, KC])
        modS = sb("modS", [P, 2, 2, KC])
        fence = sb("fence", [P, 1])
        kmax = sb("kmax", [P, KC])
        ksum = sb("ksum", [P, KC])
        rksum = sb("rksum", [P, KC])
        qmax = sb("qmax", [P, NT, H1, 1])
        qsum = sb("qsum", [P, NT, H1, 1])
        rqsum = sb("rqsum", [P, NT, H1, 1])
        att = sb("att", [P, KC, P])

        zs = work[:, 0:2048].rearrange("p (t d) -> p t d", d=D)
        hT = work[:, 2048:4096].rearrange("p (k n) -> p k n", k=KC)
        rest = work[:, 4096:5120].rearrange("p (u n) -> p u n", n=HALF)
        rest2 = work[:, 5120:6144].rearrange("p (u n) -> p u n", n=HALF)
        vtmp = work[:, 6144:6656].rearrange("p (u d) -> p u d", d=D)
        prob = work[:, :].rearrange("p (u j n) -> p u j n", u=2, j=GH)
        early = y_all[:, 0:3].rearrange("p g t c -> p (g t c)")
        wqk = early[:, 0:KC * HG * P].rearrange("p (k g c) -> p k g c", k=KC, g=HG)
        wv0 = early[:, 1024:1024 + KC * D].rearrange("p (k c) -> p k c", k=KC)
        late = parts[:, :].rearrange("p g r n -> p (g r n)").bitcast(F32)
        w1 = late[:, 0:2048].rearrange("p (w k c) -> p w k c", w=4, k=KC)
        embw = late[:, 2048:6144].rearrange("p (l e c) -> p l e c", l=2, e=EC)
        kE = late[:, 2048:4096].rearrange("p (k n) -> p k n", k=KC)
        kN = late[:, 4096:6144].rearrange("p (t d) -> p t d", d=D)
        v1 = late[:, 6144:8192].rearrange("p (t d) -> p t d", d=D)
        q1 = late[:, 8192:10240].rearrange("p (t d) -> p t d", d=D)
        qT = late[:, 10240:12288].rearrange("p (k n) -> p k n", k=KC)
        mrows1 = ks[:, 2].rearrange("p j n -> p (j n)").bitcast(F32)
        tmp1 = qs[:, 2].rearrange("p j n -> p (j n)").bitcast(F32)[:, 0:D]

        bank = [ctx.enter_context(nc.psum_tensor(f"bank{i}", [P, 2 * HALF], F32)) for i in range(4)]
        B8 = [bank[i // 2][:, (i % 2) * HALF:(i % 2 + 1) * HALF] for i in range(8)]
        sT = bank[0:2]
        sN = B8[4:6]
        acc = bank[3]

        vec_in, x_in, w_in, wo_in, mask_in = sem("vec_in"), sem("x_in"), sem("w_in"), sem("wo_in"), sem("mask_in")
        mask_out, parts_out, stack_in, cmax_out, cmax_in, late_in, stored = sem("mask_out"), sem("parts_out"), sem("stack_in"), sem("cmax_out"), sem("cmax_in"), sem("late_in"), sem("stored")
        ident_ready, ones_ready, krows_ready, qrows_ready, blocks_ready = sem("ident_ready"), sem("ones_ready"), sem("krows_ready"), sem("qrows_ready"), sem("blocks_ready")
        vecT_ready, cols_ready, msplit_step, mparts_ready = sem("vecT_ready"), sem("cols_ready"), sem("msplit_step"), sem("mparts_ready")
        ln_step, var_ready, std_ready, z_ready = sem("ln_step"), sem("var_ready"), sem("std_ready"), sem("z_ready")
        zT_ready, hT_ready = sem("zT_ready"), sem("hT_ready")
        pj_ready, pj_read = sem("pj_ready"), sem("pj_read")
        part1_ready, part2_ready, part3_ready = sem("part1_ready"), sem("part2_ready"), sem("part3_ready")
        v_ready = sem("v_ready")
        biased = sem("biased")
        sN_ready, sN_read = sem("sN_ready"), sem("sN_read")
        neg_ready, csplit_step, cparts_ready = sem("neg_ready"), sem("csplit_step"), sem("cparts_ready")
        sT_ready, exp_done, vs_ready, pv_done = sem("sT_ready"), sem("exp_done"), sem("vs_ready"), sem("pv_done")
        yT_ready, rden_ready = sem("yT_ready"), sem("rden_ready")
        scond_ready, emb_ready, mod_step, mod_ready, modS_ready, mrows_ready = sem("scond_ready"), sem("emb_ready"), sem("mod_step"), sem("mod_ready"), sem("modS_ready"), sem("mrows_ready")
        kmax_ready, kexp_ready, rk_ready, rq_ready = sem("kmax_ready"), sem("kexp_ready"), sem("rk_ready"), sem("rq_ready")
        v1_ready, q_step, qsub_ready, qexp_ready = sem("v1_ready"), sem("q_step"), sem("qsub_ready"), sem("qexp_ready")

        mask_rows = nc.dram_tensor("mask_rows", [PARTS, B, T], BF16, kind="Internal").ap()
        part_rows = nc.dram_tensor("part_rows", [G, P, PARTS, T], BF16, kind="Internal").ap()
        max_rows = nc.dram_tensor("max_rows", [PARTS, GH, T], BF16, kind="Internal").ap()

        block = ctx.enter_context(nc.Block())

        def tiles(ap):
            return ap.rearrange("b (t p) d -> p (b t) d", p=P)

        AHEAD = UNITS // NH
        RING_UNITS = MAXES + 2 + NH
        TURNS = NT * (GH * NH + NH)

        def ring_plan(with_y, with_max, more):
            units = [("max", 1, m) for m in range(AHEAD, MAXES)] if with_max else []
            if with_y:
                y_at = min(len(units), RING_UNITS // 3)
                units[y_at:y_at] = [("y", -1, n) for n in range(NH)]
            if with_max:
                units += [("max", 2, m) for m in range(4 if more else 0)] + [("neg", 1, 0)] + [("max", 2, m) for m in range(4, AHEAD if more else 0)]
            i, plan = 0, []
            for kind, dg, m in units:
                plan.append((i if with_max else RING_UNITS // 3 + i, kind, dg, m))
                i += 2 if kind == "neg" else 1
            return plan

        def ring_start(g):
            head = MAXES + 2 + AHEAD
            if isinstance(g, int):
                per = [RING_UNITS - NH] + [RING_UNITS] * (G - 3) + [RING_UNITS - AHEAD] + [NH]
                return head + sum(per[:g])
            return g * RING_UNITS + (head - NH)

        def group_channels(y, t):
            return y[:, :, t, :]

        STACKS = 2 * len(Q_PART) + 1

        @block.sync
        def _(sp):
            def rows(name, src, n):
                sp.dma_start(vecs[COL[name]:COL[name] + n, :], src.rearrange("(r p) -> r p", p=P)).then_inc(vec_in, 16)

            for name, src, n in (("norm_w", norm_w, KC), ("norm_b", norm_b, KC), ("sb_w", sb_norm_w, KC), ("sb_b", sb_norm_b, KC),
                                 ("emb_b0", emb_b, 2 * KC), ("ln_w", ln_w, KC), ("ln_b", ln_b, KC), ("bk", bk, KC),
                                 ("ln2_w", ln2_w, KC), ("ln2_b", ln2_b, KC), ("emb_b1", b_emb, 2 * KC)):
                rows(name, src, n)
            for side, src in enumerate((q_b, k_b)):
                sp.dma_start(vecs[COL["qk_b"]:COL["qk_b"] + HG, side * GC:(side + 1) * GC],
                             src.rearrange("(g c) -> g c", c=GC)).then_inc(vec_in, 16)
            rows("cond", cond.rearrange("b e -> (b e)"), B * EC)
            rows("mask0", mask0.rearrange("b t -> (b t)"), B * NT)
            rows("mask1", mask1.rearrange("b t o -> (b t o)"), B * NT)
            sp.dma_start(xs[:, 0:NT, :], tiles(x)[:, 0:NT, :]).then_inc(x_in, 16)
            sp.dma_start(mrow[:, :], mask0.rearrange("b (t p) -> (b t) p", p=P)).then_inc(mask_in, 16)
            for kc in range(KC):
                for side, src in enumerate((q_w, k_w)):
                    sp.dma_start(wqk[:, kc, :, side * GC:(side + 1) * GC],
                                 src[kc * P:(kc + 1) * P, :].rearrange("p (g c) -> p g c", c=GC)).then_inc(w_in, 16)
            sp.dma_start(wv0, v_w.rearrange("(k p) c -> p k c", p=P)).then_inc(w_in, 16)
            for i, src in enumerate((v_b, out_b, bq, bv, b_out)):
                sp.dma_start(bias_rows[:, i, :], src.partition_broadcast(P)).then_inc(w_in, 16)
            sp.wait_ge(x_in, 16)
            sp.dma_start(xs[:, NT:, :], tiles(x)[:, NT:, :]).then_inc(x_in, 16)
            sp.dma_start(wo0[:, :, :], out_w.rearrange("(k p) c -> p k c", p=P)).then_inc(wo_in, 16)
            sp.wait_ge(mparts_ready, 1)
            sp.dma_start(mask_rows.rearrange("r b (t p) -> (b t) r p", p=P), mparts[:, :, :]).then_inc(mask_out, 16)

            def stack(g, slot):
                for side, (dst, order) in enumerate(((qs, Q_PART), (ks, K_PART))):
                    for r, part in enumerate(order):
                        sp.dma_start(dst[r * DH0:(r + 1) * DH0, slot, :, :],
                                     part_rows[g, side * GC:(side + 1) * GC, part, :].rearrange("(j p) n -> p j n", p=DH0)).then_inc(stack_in, 16)
                sp.dma_start(ks[ROW_MASK:ROW_MAX, slot, :, :],
                             mask_rows[:, g // HG, :].unsqueeze(1).to_broadcast([PARTS, GH, T])).then_inc(stack_in, 16)

            def load_max(g, slot):
                sp.wait_ge(cparts_ready, g + 1)
                sp.dma_start(max_rows.rearrange("r j (t p) -> (j t) r p", p=P), cparts[:, :, :]).then_inc(cmax_out, 16)
                sp.wait_ge(cmax_out, (g + 1) * 16)
                sp.dma_start(qs[ROW_MAX:ROWS, slot, :, :], max_rows).then_inc(cmax_in, 16)

            sp.wait_ge(mask_out, 16)
            sp.wait_ge(krows_ready, 1)
            sp.wait_ge(qrows_ready, 1)
            for g in range(HG):
                sp.wait_ge(part3_ready, (g + 1) * NH)
                sp.dma_start(part_rows[g], parts[:, g]).then_inc(parts_out, 16)
                if g < 2:
                    sp.wait_ge(parts_out, 16 * (g + 1))
                    stack(g, g)
                    sp.wait_ge(stack_in, (g + 1) * 16 * STACKS)
            for g in range(HG, G):
                sp.wait_ge(part3_ready, (g + 1) * NH)
                sp.dma_start(part_rows[g], parts[:, g]).then_inc(parts_out, 16)
            load_max(0, 0)
            sp.wait_ge(parts_out, 16 * G)

            def serve(g, refill):
                if refill:
                    sp.wait_ge(stack_in, (g + 2) * (16 * STACKS))
                    sp.wait_ge(sT_ready, g * UNITS + 4)
                    stack(g + 2, sp.snap((g + 2) % SLOTS))
                load_max(g + 1, sp.snap((g + 1) % SLOTS) if refill else (g + 1) % SLOTS)

            with sp.Fori(0, G - 2) as g:
                serve(g, True)
            sp.wait_ge(stack_in, G * 16 * STACKS)
            for i, src in enumerate((Wq, Wk, Wv, W_out)):
                sp.dma_start(w1[:, i], src.rearrange("(k p) c -> p k c", p=P)).then_inc(late_in, 16)
            for i, src in enumerate((emb_w, W_emb)):
                sp.dma_start(embw[:, i], src.rearrange("(e p) c -> p e c", p=P)).then_inc(late_in, 16)
            sp.wait_ge(sT_ready, (G - 2) * UNITS + 4)
            sp.dma_start(mrows1, mask1.rearrange("b t o -> (b t o)").partition_broadcast(P)).then_inc(late_in, 16)
            serve(G - 2, False)
            with sp.Fori(0, B) as b:
                sp.wait_ge(pj_read, RING + B * UNITS_A + (b + 1) * UNITS_CD)
                sp.dma_start(tiles(out)[:, bass.ds(b * NT, NT), :], xs[:, bass.ds(b * NT, NT), :]).then_inc(stored, 16)
            sp.wait_ge(stored, B * 16)

        @block.gpsimd
        def _(pool):
            pool.memset(ident[:, :], 0.0).then_inc(ident_ready, 1)
            pool.wait_ge(ident_ready, 1)
            pool.affine_select(out=ident[:, :], in_=ident[:, :], compare_op=ALU.not_equal, fill=1.0, base=0,
                               pattern=[[-1, P]], channel_multiplier=1).then_inc(ident_ready, 1)
            pool.wait_ge(ident_ready, 2)
            pool.memset(ks[96:P, :, :, :], 1.0).then_inc(krows_ready, 1)
            pool.wait_ge(krows_ready, 1)
            pool.memset(vs[:, :, :, DH0:32], 1.0).then_inc(ones_ready, 1)
            pool.memset(blocks[:, :], 0.0).then_inc(blocks_ready, 1)
            pool.wait_ge(blocks_ready, 1)
            for j in range(P // DH1):
                pool.wait_ge(blocks_ready, 1 + j)
                pool.memset(blocks[j * DH1:(j + 1) * DH1, j * DH1:(j + 1) * DH1], 1.0).then_inc(blocks_ready, 1)
            pool.wait_ge(blocks_ready, 1 + P // DH1)
            with pool.Fori(0, B) as b:
                for u in range(HG * NH):
                    hg, n = u // NH, u % NH
                    pool.wait_ge(part2_ready, b * (HG * NH) + u + 1)
                    pool.tensor_tensor(parts[:, b * HG + hg, 2, n * HALF:(n + 1) * HALF], rest[:, u % 2, :],
                                       parts[:, b * HG + hg, 1, n * HALF:(n + 1) * HALF], op=ALU.subtract).then_inc(part3_ready, 1)
            pool.wait_ge(w_in, 16 * (2 * KC + 1 + 5))
            pool.wait_ge(z_ready, B * NT)
            for b in range(B):
                pool.tensor_tensor(xs[:, b * NT:(b + 1) * NT, :], xs[:, b * NT:(b + 1) * NT, :],
                                   bias_rows[:, 1:2, :].to_broadcast([P, NT, D]), op=ALU.add).then_inc(biased, 1)

            def stage_values(g):
                if not isinstance(g, int):
                    pool.wait_ge(pv_done, g * NT)
                pool.tensor_copy(vs[:, :, :, 0:DH0], v_all[:, g, :, :].rearrange("p t (j c) -> p t j c", j=GH)).then_inc(vs_ready, 1)

            pool.wait_ge(v_ready, B * NT)
            pool.wait_ge(ones_ready, 1)
            stage_values(0)
            with pool.Fori(1, G) as g:
                stage_values(g)
            with pool.Fori(0, B) as b:
                pool.wait_ge(z_ready, B * NT + b * 3 * NT + 2 * NT)
                xb = xs[:, bass.ds(b * NT, NT), :]
                pool.tensor_tensor(xb, xb, bias_rows[:, 4:5, :].to_broadcast([P, NT, D]), op=ALU.add).then_inc(biased, 1)

        @block.scalar
        def _(act):
            def ln_tail(L, A, Bc, func):
                act.wait_ge(var_ready, L + 1)
                act.activation(std[:, :], var[:, :], ACT.Sqrt).then_inc(std_ready, 1)
                for i in range(LN_BANKS):
                    q, kc = i // KC, i % KC
                    act.wait_ge(zT_ready, L * LN_BANKS + i + 1)
                    act.activation(hT[:, kc, q * HALF:(q + 1) * HALF], B8[i], func, scale=A(kc), bias=Bc(kc)).then_inc(hT_ready, 1)

            def col(name, i):
                return cols[:, COL[name] + i:COL[name] + i + 1]

            act.wait_ge(cols_ready, 1)
            with act.Fori(0, B) as b:
                ln_tail(b, lambda kc: col("norm_w", kc), lambda kc: col("norm_b", kc), ACT.Identity)
                for u in range(HG * NH):
                    hg, n = u // NH, u % NH
                    dst = parts[:, b * HG + hg, :, n * HALF:(n + 1) * HALF]
                    act.wait_ge(pj_ready, b * UNITS_A + u + 1)
                    act.activation(dst[:, 0, :], B8[4 + u % 4], ACT.Identity, bias=col("qk_b", hg)).then_inc(part1_ready, 1)
                    act.wait_ge(pj_read, RING + b * UNITS_A + u + 1)
                    act.activation(dst[:, 1, :], rest[:, u % 2, :], ACT.Copy).then_inc(part2_ready, 1)
                for i in range(NT):
                    act.wait_ge(pj_read, RING + b * UNITS_A + HG * NH + i + 1)
                    act.activation(v_all[:, bass.ds(b * HG, HG), i, :], vtmp[:, i % 2, :].rearrange("p (g c) -> p g c", g=HG), ACT.Copy,
                                   scale=cols[:, bass.ds(COL["mask0"] + i + b * NT, 1)]).then_inc(v_ready, 1)

            def attend(g, first=False):
                for u in range(UNITS):
                    c, j = u // GH, u % GH
                    act.wait_ge(sT_ready, g * UNITS + u + 1)
                    if j == 0 and c >= 2:
                        act.wait_ge(pv_done, g * NT + c - 1)
                    if j == 0 and c < 2 and not first:
                        act.wait_ge(pv_done, (g - 1) * NT + NT - 1 + c)
                    act.activation(prob[:, c % 2, j, :], sT[u % 2][:, :], ACT.Exp).then_inc(exp_done, 1)
                    if u == GH - 1 and not first:
                        finish(g - 1)

            def finish(g):
                act.wait_ge(pv_done, (g + 1) * NT)
                act.activation(yT[:, :], acc[:, :], ACT.Copy).then_inc(yT_ready, 1)

            act.wait_ge(part3_ready, G * NH)
            attend(0, True)
            with act.Fori(1, G) as g:
                attend(g)
            finish(G - 1)

            act.activation(scond[:, :, :], cols[:, COL["cond"]:COL["cond"] + B * EC], ACT.Silu).then_inc(scond_ready, 1)
            act.wait_ge(mod_ready, 2 * KC)
            with act.Fori(0, B) as b:
                L = B + 3 * b
                at = B * UNITS_A + b * UNITS_CD
                act.wait_ge(modS_ready, 2 * b + 2)
                ln_tail(L, lambda kc: modS[:, 0, 0, kc:kc + 1], lambda kc: modS[:, 1, 0, kc:kc + 1], ACT.Silu)
                ln_tail(L + 1, lambda kc: col("ln_w", kc), lambda kc: col("ln_b", kc), ACT.Identity)
                for kc in range(KC):
                    act.wait_ge(kmax_ready, b * KC + kc + 1)
                    act.activation(kE[:, kc, :], kE[:, kc, :], ACT.Exp, bias=kmax[:, kc:kc + 1], accum_out=ksum[:, kc:kc + 1]).then_inc(kexp_ready, 1)
                for i in range(NT):
                    act.wait_ge(pj_read, RING + at + NT + KC * NH + i + 1)
                    act.activation(v1[:, i, :], v1[:, i, :], ACT.Copy, scale=cols[:, bass.ds(COL["mask1"] + i + b * NT, 1)]).then_inc(v1_ready, 1)
                for s in range(2):
                    act.wait_ge(qsub_ready, 2 * b + s + 1)
                    half = q1[:, s * NT // 2:(s + 1) * NT // 2, :]
                    act.activation(half, half, ACT.Exp).then_inc(qexp_ready, 1)
                ln_tail(L + 2, lambda kc: modS[:, 0, 1, kc:kc + 1], lambda kc: modS[:, 1, 1, kc:kc + 1], ACT.Silu)

        @block.tensor
        def _(pe):
            def ln_transposes(L):
                for q in range(NT // 4):
                    for kc in range(KC):
                        if kc == 0:
                            pe.wait_ge(z_ready, L * NT + 4 * q + 4)
                        for t in range(4):
                            last = pe.transpose(B8[q * KC + kc][:, t * P:(t + 1) * P], zs[:, 4 * q + t, kc * P:(kc + 1) * P], ident[:, :])
                        last.then_inc(zT_ready, 1)

            def product(unit, base, pieces, used=False):
                pe.wait_ge(pj_read, base + unit + 1)
                for i, (o, l, r) in enumerate(pieces):
                    last = pe.matmul(o, l, r, start=(i == 0), stop=(i == len(pieces) - 1))
                last.then_inc(pj_ready, 1)
                return last

            def rows_times(w, t, o):
                return [(o[:, 0:D], hT[:, kc, t * P:(t + 1) * P], w[:, kc, :]) for kc in range(KC)]

            pe.wait_ge(vec_in, 16 * 16)
            pe.wait_ge(ident_ready, 2)
            pe.transpose(B8[7][:, 0:NV], vecs[:, :], ident[0:NV, 0:NV]).then_inc(vecT_ready, 1)
            pe.wait_ge(cols_ready, 1)
            pe.wait_ge(w_in, 16 * (2 * KC + 1 + 5))
            with pe.Fori(0, B) as b:
                ln_transposes(b)
                pe.wait_ge(hT_ready, (b + 1) * LN_BANKS)
                for u in range(HG * NH):
                    hg, n = u // NH, u % NH
                    o = B8[4 + u % 4]
                    product(u, b * UNITS_A, [(o, wqk[:, kc, hg, :], hT[:, kc, n * HALF:(n + 1) * HALF]) for kc in range(KC)])
                for i in range(NT):
                    u = HG * NH + i
                    last = product(u, b * UNITS_A, rows_times(wv0, i, B8[4 + u % 4]))

            def fill(kind, g, m, slot, at, i):
                o = sN[i % 2]
                if not isinstance(at, int) or at + i >= 2:
                    pe.wait_ge(sN_read, at + i - 1)
                if kind == "max":
                    r, n = m // NH, m % NH
                    j, qt = r // NT, r % NT
                    pe.matmul(o, qs[0:ROW_MAX, slot, j, qt * P:(qt + 1) * P], ks[0:ROW_MAX, slot, j, n * HALF:(n + 1) * HALF],
                              start=True, stop=True).then_inc(sN_ready, 1)
                elif kind == "y":
                    pe.wait_ge(yT_ready, g + 1)
                    for t in range(4):
                        last = pe.transpose(o[:, t * P:(t + 1) * P], yT[:, (4 * m + t) * P:(4 * m + t + 1) * P], ident[:, :])
                    last.then_inc(sN_ready, 1)
                else:
                    pe.wait_ge(neg_ready, g + 1)
                    pe.transpose(o[0:UNITS, 0:P], negmax[:, :], ident[:, :]).then_inc(sN_ready, 2)

            def values(g, c, n):
                if n == 0:
                    pe.wait_ge(exp_done, g * UNITS + (c + 1) * GH)
                    if c == 0:
                        pe.wait_ge(vs_ready, g + 1)
                        if not isinstance(g, int) or g > 0:
                            pe.wait_ge(yT_ready, g)
                for j in range(GH):
                    last = pe.matmul(acc[32 * j:32 * j + 32, n * HALF:(n + 1) * HALF], vs[:, c, j, :], prob[:, c % 2, j, n * HALF:(n + 1) * HALF],
                                     start=(c == 0), stop=(c == NT - 1), skip_group_check=True)
                if n == NH - 1:
                    last.then_inc(pv_done, 1)

            def attend(g, slots, first=False, last_group=False, more=True):
                at = ring_start(g)
                plan = ring_plan(not first, not last_group, more)
                pe.wait_ge(cmax_in, (g + 1) * 16)
                if not last_group:
                    pe.wait_ge(stack_in, (g + 2) * (16 * STACKS))
                turn = done = 0

                def turns(k):
                    nonlocal turn, done
                    turn += k
                    while done < len(plan) and plan[done][0] * TURNS < turn * RING_UNITS:
                        i, kind, dg, m = plan[done]
                        if kind == "max" and dg == 2 and m == 0:
                            pe.wait_ge(stack_in, (g + 3) * (16 * STACKS))
                        fill(kind, g + dg, m, slots[max(dg, 0)], at, m if last_group else i)
                        done += 1

                for c in range(NT):
                    for j in range(GH):
                        u = c * GH + j
                        if u >= 2 or not first:
                            pe.wait_ge(exp_done, g * UNITS + u - 1)
                        for n in range(NH):
                            last = pe.matmul(sT[u % 2][:, n * HALF:(n + 1) * HALF], ks[0:ROWS, slots[0], j, c * P:(c + 1) * P],
                                             qs[0:ROWS, slots[0], j, n * HALF:(n + 1) * HALF], start=True, stop=True)
                            if n == NH - 1:
                                last.then_inc(sT_ready, 1)
                            turns(1)
                        if c > 0 and j >= GH - NH:
                            values(g, c - 1, j - (GH - NH))
                            turns(1)
                        if c == 0 and not first and 1 <= j <= NH:
                            values(g - 1, NT - 1, j - 1)
                            turns(1)
                assert first or turn == TURNS
                turns(TURNS)
                assert done == len(plan)

            pe.wait_ge(pj_read, RING + B * UNITS_A)
            pe.wait_ge(stack_in, 16 * STACKS)
            for i in range(MAXES):
                fill("max", 0, i, 0, 0, i)
            fill("neg", 0, 0, 0, 0, MAXES)
            pe.wait_ge(stack_in, 2 * 16 * STACKS)
            for m in range(AHEAD):
                fill("max", 1, m, 1, 0, MAXES + 2 + m)
            attend(0, (0, 1, 2), first=True)
            with pe.Fori(1, G - 2) as g:
                attend(g, (pe.snap(g % SLOTS), pe.snap((g + 1) % SLOTS), pe.snap((g + 2) % SLOTS)))
            attend(G - 2, ((G - 2) % SLOTS, (G - 1) % SLOTS, 0), more=False)
            attend(G - 1, ((G - 1) % SLOTS, 0, 0), last_group=True)
            for n in range(NH):
                values(G - 1, NT - 1, n)
            for m in range(NH):
                fill("y", G - 1, m, 0, ring_start(G), m)

            pe.wait_ge(late_in, 16 * 7)
            pe.wait_ge(scond_ready, 1)
            for l in range(2):
                for oc in range(2 * KC):
                    at = (l * 2 * KC + oc) * B
                    for e in range(EC):
                        last = pe.matmul(B8[0][:, at:at + B], embw[:, l, e, oc * P:(oc + 1) * P], scond[:, :, e],
                                         start=(e == 0), stop=(e == EC - 1))
            last.then_inc(emb_ready, 1)
            pe.wait_ge(mod_step, 2 * 2 * KC)
            BASE = B * UNITS_A
            with pe.Fori(0, B) as b:
                L = B + 3 * b
                at = BASE + b * UNITS_CD
                u = 0

                def ring():
                    return B8[4 + u % 4]

                ln_transposes(L)
                pe.wait_ge(hT_ready, (L + 1) * LN_BANKS)
                for t in range(NT):
                    last = product(u, at, rows_times(wo0, t, ring()))
                    u += 1

                ln_transposes(L + 1)
                pe.wait_ge(hT_ready, (L + 2) * LN_BANKS)
                for kc in range(KC):
                    for n in range(NH):
                        product(u, at, [(ring(), w1[:, 1, i, kc * P:(kc + 1) * P], hT[:, i, n * HALF:(n + 1) * HALF]) for i in range(KC)])
                        u += 1
                for t in range(NT):
                    product(u, at, rows_times(w1[:, 2], t, ring()))
                    u += 1
                for t in range(NT):
                    product(u, at, rows_times(w1[:, 0], t, ring()))
                    u += 1
                for s in range(NT // 2):
                    if s == 0:
                        pe.wait_ge(kexp_ready, (b + 1) * KC)
                    pe.wait_ge(pj_read, at + u + 1)
                    for t in range(2):
                        for kc in range(KC):
                            last = pe.transpose(ring()[:, (t * KC + kc) * P:(t * KC + kc + 1) * P],
                                                kE[:, kc, (2 * s + t) * P:(2 * s + t + 1) * P], ident[:, :])
                    last.then_inc(pj_ready, 1)
                    u += 1
                for kc in range(KC):
                    for n in range(NH):
                        pe.wait_ge(qexp_ready, 2 * b + n + 1)
                        pe.wait_ge(pj_read, at + u + 1)
                        for t in range(4):
                            last = pe.transpose(ring()[:, t * P:(t + 1) * P], q1[:, 4 * n + t, kc * P:(kc + 1) * P], ident[:, :])
                        last.then_inc(pj_ready, 1)
                        u += 1
                pe.wait_ge(pj_read, RING + at + u)
                pe.wait_ge(v1_ready, (b + 1) * NT)
                for kc in range(KC):
                    product(u, at, [(ring()[:, 0:P], kN[:, t, kc * P:(kc + 1) * P], v1[:, t, kc * P:(kc + 1) * P]) for t in range(NT)])
                    u += 1
                pe.wait_ge(pj_read, RING + at + u)
                for t in range(NT):
                    pe.wait_ge(pj_read, at + u + 1)
                    for kc in range(KC):
                        last = pe.matmul(ring()[:, kc * P:(kc + 1) * P], qT[:, kc, t * P:(t + 1) * P], att[:, kc, :], start=True, stop=True)
                    last.then_inc(pj_ready, 1)
                    u += 1

                ln_transposes(L + 2)
                pe.wait_ge(hT_ready, (L + 3) * LN_BANKS)
                for t in range(NT):
                    product(u, at, rows_times(w1[:, 3], t, ring()))
                    u += 1
                assert u == UNITS_CD

        @block.vector
        def _(dve):
            def layer_norm(L, src):
                base = L * LN_STEPS
                for t in range(NT):
                    dve.bn_stats(stats[:, t, :], src(t)).then_inc(ln_step, 1)
                dve.wait_ge(ln_step, base + NT)
                dve.memset(fence[:, :], 0.0)
                for t in range(NT):
                    dve.bn_aggr(mv[:, t, :], stats[:, t, :]).then_inc(ln_step, 1)
                dve.wait_ge(ln_step, base + 2 * NT)
                dve.tensor_scalar_add(var[:, :], mv[:, :, 1], EPS).then_inc(var_ready, 1)
                dve.wait_ge(std_ready, L + 1)
                dve.reciprocal(rstd[:, :], std[:, :]).then_inc(ln_step, 1)
                dve.wait_ge(ln_step, base + LN_STEPS)
                for t in range(NT):
                    dst = zs[:, t, :]
                    s = src(t)
                    if len(s.shape) == 3:
                        dst = dst.rearrange("p (g c) -> p g c", g=HG)
                    dve.tensor_scalar(dst, s, mv[:, t, 0:1], rstd[:, t:t + 1], op0=ALU.subtract, op1=ALU.mult).then_inc(z_ready, 1)

            dve.memset(qs[96:P, :, :, :], 1.0).then_inc(qrows_ready, 1)
            dve.memset(negmax[:, 0:1], 0.0).then_inc(pj_read, RING)
            dve.wait_ge(vecT_ready, 1)
            dve.tensor_copy(cols[:, :], B8[7][:, 0:NV]).then_inc(cols_ready, 1)
            dve.wait_ge(mask_in, 16)
            dve.tensor_scalar(mrest[:, 0, :], mrow[:, :], 1.0, BIG, op0=ALU.subtract, op1=ALU.mult).then_inc(msplit_step, 1)
            dve.wait_ge(msplit_step, 1)
            dve.tensor_copy(mparts[:, 0, :], mrest[:, 0, :]).then_inc(msplit_step, 1)
            dve.wait_ge(msplit_step, 2)
            dve.tensor_tensor(mrest[:, 1, :], mrest[:, 0, :], mparts[:, 0, :], op=ALU.subtract).then_inc(msplit_step, 1)
            dve.wait_ge(msplit_step, 3)
            dve.tensor_copy(mparts[:, 1, :], mrest[:, 1, :]).then_inc(msplit_step, 1)
            dve.wait_ge(msplit_step, 4)
            dve.tensor_tensor(mparts[:, 2, :], mrest[:, 1, :], mparts[:, 1, :], op=ALU.subtract).then_inc(mparts_ready, 1)

            dve.wait_ge(w_in, 16 * (2 * KC + 1 + 5))
            with dve.Fori(0, B) as b:
                dve.wait_ge(x_in, (b + 1) * 16)
                layer_norm(b, lambda t: xs[:, bass.ds(b * NT + t, 1), :].rearrange("p o d -> p (o d)"))
                for u in range(HG * NH):
                    hg, n = u // NH, u % NH
                    c = COL["qk_b"] + hg
                    dve.wait_ge(part1_ready, b * (HG * NH) + u + 1)
                    if u >= 2:
                        dve.wait_ge(part3_ready, b * (HG * NH) + u - 1)
                    dve.scalar_tensor_tensor(out=rest[:, u % 2, :], in0=B8[4 + u % 4], scalar=cols[:, c:c + 1],
                                             in1=parts[:, b * HG + hg, 0, n * HALF:(n + 1) * HALF],
                                             op0=ALU.add, op1=ALU.subtract).then_inc(pj_read, 1)
                dve.wait_ge(part3_ready, (b + 1) * (HG * NH))
                for i in range(NT):
                    u = HG * NH + i
                    dve.wait_ge(pj_ready, b * UNITS_A + u + 1)
                    if i >= 2:
                        dve.wait_ge(v_ready, b * NT + i - 1)
                    dve.tensor_tensor(vtmp[:, i % 2, :], B8[4 + u % 4][:, 0:D], bias_rows[:, 0, :], op=ALU.add).then_inc(pj_read, 1)

            def read(kind, g, m, at, i):
                src = sN[i % 2]
                if kind == "neg":
                    dve.wait_ge(sN_ready, at + i + 2)
                    if not isinstance(g, int) or g > 0:
                        dve.wait_ge(cmax_out, g * 16)
                    src, base = src[0:UNITS, 0:P], g * 2
                    dve.tensor_copy(cparts[:, 0, :], src).then_inc(csplit_step, 1)
                    dve.wait_ge(csplit_step, base + 1)
                    dve.tensor_tensor(crest[:, 0, :], src, cparts[:, 0, :], op=ALU.subtract).then_inc(sN_read, 2)
                    dve.wait_ge(sN_read, at + i + 2)
                    dve.tensor_copy(cparts[:, 1, :], crest[:, 0, :]).then_inc(csplit_step, 1)
                    dve.wait_ge(csplit_step, base + 2)
                    dve.tensor_tensor(cparts[:, 2, :], crest[:, 0, :], cparts[:, 1, :], op=ALU.subtract).then_inc(cparts_ready, 1)
                    return
                dve.wait_ge(sN_ready, at + i + 1)
                if kind == "max":
                    r, n = m // NH, m % NH
                    dve.tensor_reduce(halfmax[:, r, n:n + 1], src, axis=AX.X, op=ALU.max, negate=True).then_inc(sN_read, 1)
                    if m == MAXES - 1:
                        dve.wait_ge(sN_read, at + i + 1)
                        dve.tensor_reduce(negmax[:, :], halfmax[:, :, :], axis=AX.X, op=ALU.min).then_inc(neg_ready, 1)
                        dve.wait_ge(neg_ready, g + 1)
                else:
                    src = src.rearrange("p (u c) -> p u c", c=32)
                    dve.reciprocal(rden[:, m, :, :], src[:, :, DH0:DH0 + 1]).then_inc(rden_ready, 1)
                    dve.wait_ge(rden_ready, g * NH + m + 1)
                    dve.tensor_tensor(y_all[:, g, 4 * m:4 * m + 4, :].rearrange("p t (j c) -> p (t j) c", c=DH0), src[:, :, 0:DH0],
                                      rden[:, m, :, :].to_broadcast([P, 4 * GH, DH0]), op=ALU.mult).then_inc(sN_read, 1)

            def beside(g, first=False, last_group=False, more=True):
                for i, kind, dg, m in ring_plan(not first, not last_group, more):
                    read(kind, g + dg, m, ring_start(g), i if not last_group else m)

            for i in range(MAXES):
                read("max", 0, i, 0, i)
            read("neg", 0, 0, 0, MAXES)
            for m in range(AHEAD):
                read("max", 1, m, 0, MAXES + 2 + m)
            beside(0, first=True)
            with dve.Fori(1, G - 2) as g:
                beside(g)
            beside(G - 2, more=False)
            beside(G - 1, last_group=True)
            for m in range(NH):
                read("y", G - 1, m, ring_start(G), m)

            dve.wait_ge(emb_ready, 1)
            bank_emb = B8[0][:, 0:2 * 2 * KC * B].rearrange("p (l o b) -> p l o b", l=2, b=B)
            n = 0
            for l in range(2):
                for oc in range(2 * KC):
                    c = COL[f"emb_b{l}"] + oc
                    dve.tensor_scalar(emb[:, l, oc, :], bank_emb[:, l, oc, :], cols[:, c:c + 1], None, op0=ALU.add).then_inc(mod_step, 1)
                    n += 1
            dve.wait_ge(mod_step, n)
            for l, (w, s) in enumerate((("sb_w", "sb_b"), ("ln2_w", "ln2_b"))):
                for kc in range(KC):
                    cw, cb = COL[w] + kc, COL[s] + kc
                    dve.tensor_scalar(modA[:, l, :, kc], emb[:, l, kc, :], 1.0, cols[:, cw:cw + 1], op0=ALU.add, op1=ALU.mult).then_inc(mod_step, 1)
                    dve.tensor_scalar(modB[:, l, :, kc], emb[:, l, kc, :], 1.0, cols[:, cb:cb + 1], op0=ALU.add, op1=ALU.mult).then_inc(mod_step, 1)
                    n += 2
            dve.wait_ge(mod_step, n)
            for l in range(2):
                for kc in range(KC):
                    dve.tensor_tensor(modB[:, l, :, kc], modB[:, l, :, kc], emb[:, l, KC + kc, :], op=ALU.add).then_inc(mod_ready, 1)
            dve.wait_ge(late_in, 16 * 7)
            dve.tensor_scalar(mrows1, mrows1, 1.0, BIG, op0=ALU.subtract, op1=ALU.mult).then_inc(mrows_ready, 1)
            dve.wait_ge(mrows_ready, 1)
            dve.wait_ge(mod_ready, 2 * KC)
            dve.wait_ge(blocks_ready, 1 + P // DH1)
            dve.wait_ge(biased, B)
            BASE = B * UNITS_A
            QS = 4
            with dve.Fori(0, B) as b:
                L = B + 3 * b
                at = BASE + b * UNITS_CD
                u = 0

                def ring():
                    return B8[4 + u % 4]

                def xt(t):
                    return xs[:, bass.ds(b * NT + t, 1), :].rearrange("p o d -> p (o d)")

                dve.wait_ge(sN_read, ring_start(G) + NH)
                yb = y_all[:, bass.ds(b * HG, HG)]
                dve.wait_ge(hT_ready, L * LN_BANKS)
                dve.tensor_copy(modS[:, 0, :, :], modA[:, :, bass.ds(b, 1), :].rearrange("p l o k -> p (l o) k")).then_inc(modS_ready, 1)
                dve.tensor_copy(modS[:, 1, :, :], modB[:, :, bass.ds(b, 1), :].rearrange("p l o k -> p (l o) k")).then_inc(modS_ready, 1)
                layer_norm(L, lambda t: group_channels(yb, t))
                for t in range(NT):
                    dve.wait_ge(pj_ready, at + u + 1)
                    dve.tensor_tensor(xt(t), xt(t), ring()[:, 0:D], op=ALU.add).then_inc(pj_read, 1)
                    u += 1
                dve.wait_ge(pj_read, RING + at + u)
                dve.memset(fence[:, :], 0.0)
                layer_norm(L + 1, xt)
                for kc in range(KC):
                    c = COL["bk"] + kc
                    for n in range(NH):
                        dve.wait_ge(pj_ready, at + u + 1)
                        dve.scalar_tensor_tensor(out=kE[:, kc, n * HALF:(n + 1) * HALF], in0=ring(), scalar=cols[:, c:c + 1],
                                                 in1=mrows1[:, bass.ds(b * T + n * HALF, HALF)], op0=ALU.add, op1=ALU.add).then_inc(pj_read, 1)
                        u += 1
                    dve.wait_ge(pj_read, RING + at + u)
                    dve.tensor_reduce(kmax[:, kc:kc + 1], kE[:, kc, :], axis=AX.X, op=ALU.max, negate=True).then_inc(kmax_ready, 1)
                for t in range(NT):
                    dve.wait_ge(pj_ready, at + u + 1)
                    dve.tensor_tensor(v1[:, t, :], ring()[:, 0:D], bias_rows[:, 3, :], op=ALU.add).then_inc(pj_read, 1)
                    u += 1
                qb = b * 4
                for t in range(NT):
                    dve.wait_ge(pj_ready, at + u + 1)
                    dve.tensor_tensor(q1[:, t, :], ring()[:, 0:D], bias_rows[:, 2, :], op=ALU.add).then_inc(pj_read, 1)
                    u += 1
                dve.wait_ge(pj_read, RING + at + u)
                hb = NT // 2
                for s in range(2):
                    qh = q1[:, s * hb:(s + 1) * hb, :].rearrange("p t (h c) -> p (t h) c", c=DH1)
                    mx = qmax[:, s * hb:(s + 1) * hb].rearrange("p t h o -> p (t h) o")
                    dve.tensor_reduce(mx, qh, axis=AX.X, op=ALU.max).then_inc(q_step, 1)
                    dve.wait_ge(q_step, qb + s + 1)
                    dve.tensor_tensor(qh, qh, mx.to_broadcast([P, hb * H1, DH1]), op=ALU.subtract).then_inc(qsub_ready, 1)
                for s in range(2):
                    qh = q1[:, s * hb:(s + 1) * hb, :].rearrange("p t (h c) -> p (t h) c", c=DH1)
                    sm = qsum[:, s * hb:(s + 1) * hb].rearrange("p t h o -> p (t h) o")
                    dve.wait_ge(qexp_ready, 2 * b + s + 1)
                    dve.tensor_reduce(sm, qh, axis=AX.X, op=ALU.add).then_inc(q_step, 1)
                dve.wait_ge(q_step, qb + 4)
                dve.reciprocal(rqsum[:, :, :, :], qsum[:, :, :, :]).then_inc(rq_ready, 1)
                for s in range(NT // 2):
                    dve.wait_ge(pj_ready, at + u + 1)
                    dve.tensor_copy(kN[:, 2 * s:2 * s + 2, :].rearrange("p t d -> p (t d)"), ring()).then_inc(pj_read, 1)
                    u += 1
                for kc in range(KC):
                    for n in range(NH):
                        dve.wait_ge(pj_ready, at + u + 1)
                        dve.tensor_copy(qT[:, kc, n * HALF:(n + 1) * HALF], ring()).then_inc(pj_read, 1)
                        u += 1
                dve.wait_ge(kexp_ready, (b + 1) * KC)
                dve.reciprocal(rksum[:, :], ksum[:, :]).then_inc(rk_ready, 1)
                dve.wait_ge(rk_ready, b + 1)
                for kc in range(KC):
                    dve.wait_ge(pj_ready, at + u + 1)
                    dve.scalar_tensor_tensor(out=att[:, kc, :], in0=ring()[:, 0:P], scalar=rksum[:, kc:kc + 1], in1=blocks[:, :],
                                             op0=ALU.mult, op1=ALU.mult).then_inc(pj_read, 1)
                    u += 1
                dve.wait_ge(rq_ready, b + 1)
                for t in range(NT):
                    dve.wait_ge(pj_ready, at + u + 1)
                    dve.tensor_tensor(q1[:, t, :].rearrange("p (h c) -> p h c", c=DH1), ring()[:, 0:D].rearrange("p (h c) -> p h c", c=DH1),
                                      rqsum[:, t].to_broadcast([P, H1, DH1]), op=ALU.mult).then_inc(pj_read, 1)
                    u += 1
                dve.wait_ge(pj_read, RING + at + u)
                layer_norm(L + 2, lambda t: q1[:, t, :])
                dve.wait_ge(biased, B + b + 1)
                for t in range(NT):
                    dve.wait_ge(pj_ready, at + u + 1)
                    dve.tensor_tensor(xt(t), xt(t), ring()[:, 0:D], op=ALU.add).then_inc(pj_read, 1)
                    u += 1
                assert u == UNITS_CD


_INS = ["x", "cond_2048", "mask_BxS_ff1", "mask_BxSx1_fk1",
        "L0_cond_norm_w", "L0_cond_norm_b", "L0_cond_q_w", "L0_cond_q_b", "L0_cond_k_w", "L0_cond_k_b", "L0_cond_v_w", "L0_cond_v_b",
        "L0_cond_emb_w", "L0_cond_emb_b", "L0_cond_sb_norm_w", "L0_cond_sb_norm_b", "L0_cond_out_w", "L0_cond_out_b",
        "L1_cond_ln_w", "L1_cond_ln_b", "L1_cond_Wq", "L1_cond_bq", "L1_cond_Wk", "L1_cond_bk", "L1_cond_Wv", "L1_cond_bv",
        "L1_cond_W_emb", "L1_cond_b_emb", "L1_cond_ln2_w", "L1_cond_ln2_b", "L1_cond_W_out", "L1_cond_b_out"]


def kernel(**inputs):
    import concourse.bacc as bacc
    from concourse.bass_utils import run_bass_kernel_spmd

    nc = bacc.Bacc("TRN2", target_bir_lowering=False, num_devices=1)
    arrays, args = {}, []
    for name in _INS:
        a = np.ascontiguousarray(inputs[name])
        arrays[f"in_{name}"] = a
        args.append(nc.dram_tensor(f"in_{name}", a.shape, mybir.dt.from_np(a.dtype), kind="ExternalInput").ap())
    shape = arrays["in_x"].shape
    args.append(nc.dram_tensor("out_x", shape, mybir.dt.float32, kind="ExternalOutput").ap())
    two_layer_conditioned_attention(nc, *args)
    r = run_bass_kernel_spmd(nc, [arrays], core_ids=[0])
    return r.results[0]["out_x"]
```

```python
from contextlib import ExitStack

import numpy as np
import concourse.bass as bass
from concourse import mybir


def two_layer_conditioned_attention(
    nc: bass.Bass,
    x, cond, mask0, mask1,
    norm_w, norm_b, q_w, q_b, k_w, k_b, v_w, v_b, emb_w, emb_b, sb_norm_w, sb_norm_b, out_w, out_b,
    ln_w, ln_b, Wq, bq, Wk, bk, Wv, bv, W_emb, b_emb, ln2_w, ln2_b, W_out, b_out,
    out,
):
    F32, BF16 = mybir.dt.float32, mybir.dt.bfloat16
    ALU, ACT, AX = mybir.AluOpType, mybir.ActivationFunctionType, mybir.AxisListType

    B, T, D = x.shape
    P = 128
    NT = T // P
    KC = D // P
    HALF = 512
    NH = T // HALF
    H0, H1 = 16, 8
    DH0, DH1 = D // H0, D // H1
    GH = 4
    GC = GH * DH0
    HG = H0 // GH
    G = B * HG
    E = cond.shape[1]
    EC = E // P
    EPS = 1e-5
    BIG = 1e6
    BF16_ONES = float(np.array([0x3F803F80], np.uint32).view(np.float32)[0])

    Q_PART = [0, 0, 0, 1, 1, 2]
    K_PART = [0, 1, 2, 0, 1, 0]
    PARTS = 3
    ROW_MASK = len(Q_PART) * DH0
    ROW_MAX = ROW_MASK + PARTS
    ROWS = ROW_MAX + PARTS
    SLOTS = 3

    UNITS = GH * NT
    MAXES = UNITS * NH

    names = ["norm_w", "norm_b", "qk_b", "mask0",
             "sb_w", "sb_b", "emb_b0", "ln_w", "ln_b", "bk", "ln2_w", "ln2_b", "emb_b1", "cond", "mask1"]
    sizes = [KC, KC, HG, B * NT, KC, KC, 2 * KC, KC, KC, KC, KC, KC, 2 * KC, B * EC, B * NT]
    COL = dict(zip(names, np.concatenate([[0], np.cumsum(sizes)[:-1]]).astype(int).tolist()))
    NV, NV0 = sum(sizes), COL["sb_w"]

    LN_STEPS = 2 * NT + 1
    TURN = (NT // 4) * KC
    RING = 4
    UNITS_A = HG * NH + NT // 2
    STAGES = {"out0": NT // 2, "keys": KC * NH, "queries": NT // 2, "values": NT // 2, "att": KC, "y": NT // 2, "out1": NT // 2}

    def stage_start(stage, b):
        n = B * UNITS_A
        for name, units in STAGES.items():
            if name == stage:
                return n + b * units
            n += B * units

    LN = {(kind, b): i * B + b for i, kind in enumerate(("in0", "mid0", "in1", "mid1")) for b in range(B)}
    turns_order = [("in0", b) for b in range(B)] + [("mid0", b) for b in range(B)] + [("in1", b) for b in range(B)]
    turns_order += [(kind, b) for b in range(B) for kind in ("kT", "qT")] + [("mid1", b) for b in range(B)]
    TURN_NO = {key: i for i, key in enumerate(turns_order)}

    ctx = ExitStack()
    with ctx:
        def sb(name, shape, dt=F32):
            return ctx.enter_context(nc.sbuf_tensor(name, shape, dt))

        def sem(name):
            return ctx.enter_context(nc.semaphore(name))

        xs = sb("xs", [P, B * NT, D])
        work = sb("work", [P, 8192])
        parts = sb("parts", [P, G, PARTS, T], BF16)
        qs = sb("qs", [P, SLOTS, GH, T], BF16)
        ks = sb("ks", [P, SLOTS, GH, T], BF16)
        v_all = sb("v_all", [P, G, NT, GC])
        vs = sb("vs", [P, NT, GH, 32])
        y_all = sb("y_all", [P, G, NT, GC])
        yT = sb("yT", [P, T])
        bias_rows = sb("bias_rows", [P, 5, D])
        wo0 = sb("wo0", [P, KC, D])
        ident = sb("ident", [P, P])
        blocks = sb("blocks", [P, P])
        vecs = sb("vecs", [NV0, P])
        vecs2 = sb("vecs2", [NV - NV0, P])
        cols = sb("cols", [P, NV])
        mrow = sb("mrow", [B * NT, P])
        mrest = sb("mrest", [B * NT, 2, P])
        mparts = sb("mparts", [B * NT, PARTS, P], BF16)
        stats = sb("stats", [P, B, NT, 6])
        mv = sb("mv", [P, B, NT, 2])
        var = sb("var", [P, B, NT])
        std = sb("std", [P, B, NT])
        rstd = sb("rstd", [P, B, NT])
        halfmax = sb("halfmax", [P, UNITS, NH])
        negmax = sb("negmax", [P, UNITS])
        crest = sb("crest", [UNITS, 1, P])
        cparts = sb("cparts", [UNITS, PARTS, P], BF16)
        rden = sb("rden", [P, NH, 4 * GH, 1])
        scond = sb("scond", [P, B, EC])
        emb = sb("emb", [P, 2, 2 * KC, B])
        modA = sb("modA", [P, 2, KC, B])
        modB = sb("modB", [P, 2, KC, B])
        fence = sb("fence", [P, 1])
        kmax = sb("kmax", [P, B, KC])
        ksum = sb("ksum", [P, B, KC])
        rksum = sb("rksum", [P, B, KC])
        qmax = sb("qmax", [P, B, NT, H1, 1])
        qsum = sb("qsum", [P, B, NT, H1, 1])
        rqsum = sb("rqsum", [P, B, NT, H1, 1])
        att = sb("att", [P, B, KC, P])

        def floats(ap):
            return ap.rearrange("p a b -> p (a b)").bitcast(F32)

        def by_tile(flat):
            return flat.rearrange("p (t d) -> p t d", d=D)

        def by_channel(flat):
            return flat.rearrange("p (k n) -> p k n", k=KC)

        TD = NT * D
        late = parts[:, :].rearrange("p g r n -> p (g r n)").bitcast(F32)
        w1 = late[:, 0:4 * KC * D].rearrange("p (w k c) -> p w k c", w=4, k=KC)
        embw = late[:, 2 * TD:4 * TD].rearrange("p (l e c) -> p l e c", l=2, e=EC)
        v_flat = v_all[:, :].rearrange("p g t c -> p (g t c)")
        zs_in = [by_tile(work[:, 0:TD]), by_tile(work[:, TD:2 * TD])]
        hT = [by_channel(work[:, 2 * TD:3 * TD]), by_channel(work[:, 3 * TD:4 * TD])]
        zs = [by_tile(late[:, TD:2 * TD]), zs_in[1]]
        kE = [by_channel(late[:, 2 * TD:3 * TD]), by_channel(floats(ks[:, 0]))]
        kN = [by_tile(late[:, 3 * TD:4 * TD]), by_tile(floats(ks[:, 1]))]
        v1 = [by_tile(late[:, 4 * TD:5 * TD]), by_tile(v_flat[:, 0:TD])]
        q1 = [by_tile(late[:, 5 * TD:6 * TD]), by_tile(v_flat[:, TD:2 * TD])]
        qT = [by_channel(work[:, 0:TD]), by_channel(floats(qs[:, 0]))]
        mrows1 = floats(ks[:, 2])
        prob = work[:, :].rearrange("p (u j n) -> p u j n", u=2, j=GH)
        early = y_all[:, :].rearrange("p g t c -> p (g t c)")
        wqk = early[:, 0:KC * HG * P].rearrange("p (k g c) -> p k g c", k=KC, g=HG)
        wv0 = early[:, 1024:1024 + KC * D].rearrange("p (k c) -> p k c", k=KC)
        rest = early[:, 1536:2560].rearrange("p (u n) -> p u n", n=HALF)
        vtmp = early[:, 2560:3584].rearrange("p (u n) -> p u n", n=2 * D)

        bank = [ctx.enter_context(nc.psum_tensor(f"bank{i}", [P, 2 * HALF], F32)) for i in range(4)]
        B8 = [bank[i // 2][:, (i % 2) * HALF:(i % 2 + 1) * HALF] for i in range(8)]
        sT = bank[0:2]
        sN = B8[4:6]
        acc = bank[3]

        vec_in, vec2_in, w_in, wv_in, wo_in, mask_in = sem("vec_in"), sem("vec2_in"), sem("w_in"), sem("wv_in"), sem("wo_in"), sem("mask_in")
        x_in = [sem(f"x{b}_in") for b in range(B)]
        mask_out, parts_out, stack_in, cmax_out, cmax_in, embw_in, late_in, stored = sem("mask_out"), sem("parts_out"), sem("stack_in"), sem("cmax_out"), sem("cmax_in"), sem("embw_in"), sem("late_in"), sem("stored")
        ident_ready, ones_ready, krows_ready, qrows_ready, blocks_ready = sem("ident_ready"), sem("ones_ready"), sem("krows_ready"), sem("qrows_ready"), sem("blocks_ready")
        vecT_ready, cols_ready, msplit_step, mparts_ready = sem("vecT_ready"), sem("cols_ready"), sem("msplit_step"), sem("mparts_ready")
        ln_step, var_ready, std_ready, z_ready = sem("ln_step"), sem("var_ready"), sem("std_ready"), sem("z_ready")
        turn_ready, turn_read = sem("turn_ready"), sem("turn_read")
        pj_ready, pj_read = sem("pj_ready"), sem("pj_read")
        part1_ready, part2_ready, part3_ready = sem("part1_ready"), sem("part2_ready"), sem("part3_ready")
        v_ready = sem("v_ready")
        biased = sem("biased")
        sN_ready, sN_read = sem("sN_ready"), sem("sN_read")
        neg_ready, csplit_step, cparts_ready = sem("neg_ready"), sem("csplit_step"), sem("cparts_ready")
        sT_ready, exp_done, vs_ready, pv_done = sem("sT_ready"), sem("exp_done"), sem("vs_ready"), sem("pv_done")
        yT_ready, rden_ready = sem("yT_ready"), sem("rden_ready")
        scond_ready, emb_ready, mod_step, mod_ready, mrows_in, mrows_ready = sem("scond_ready"), sem("emb_ready"), sem("mod_step"), sem("mod_ready"), sem("mrows_in"), sem("mrows_ready")
        kmax_ready, kexp_ready, rk_ready, rq_ready = sem("kmax_ready"), sem("kexp_ready"), sem("rk_ready"), sem("rq_ready")
        v1_ready, q_step, qsub_ready, qexp_ready = sem("v1_ready"), sem("q_step"), sem("qsub_ready"), sem("qexp_ready")

        mask_rows = nc.dram_tensor("mask_rows", [PARTS, B, T], BF16, kind="Internal").ap()
        part_rows = nc.dram_tensor("part_rows", [G, P, PARTS, T], BF16, kind="Internal").ap()
        max_rows = nc.dram_tensor("max_rows", [PARTS, GH, T], BF16, kind="Internal").ap()

        block = ctx.enter_context(nc.Block())

        def tiles(ap):
            return ap.rearrange("b (t p) d -> p (b t) d", p=P)

        AHEAD = UNITS // NH
        RING_UNITS = MAXES + 2 + NH
        VALUES_TURNS = 4
        TURNS = NT * (GH * NH + VALUES_TURNS * NH)

        BESIDE_A = 3
        prologue = [("max", 0, m) for m in range(MAXES)] + [("neg", 0, 0), ("neg", 0, 1)] + [("max", 1, m) for m in range(AHEAD)]

        def prologue_share(u):
            return [(i, *prologue[i]) for i in range(u * BESIDE_A, (u + 1) * BESIDE_A)]

        def prologue_rest():
            return [(i, *prologue[i]) for i in range(UNITS_A * BESIDE_A, len(prologue))]

        def ring_plan(with_y, with_max, more):
            units = [("max", 1, m) for m in range(AHEAD, MAXES)] if with_max else []
            if with_y:
                y_at = min(len(units), RING_UNITS // 3)
                units[y_at:y_at] = [("y", -1, n) for n in range(NH)]
            if with_max:
                units += [("max", 2, m) for m in range(4 if more else 0)] + [("neg", 1, 0)] + [("max", 2, m) for m in range(4, AHEAD if more else 0)]
            i, plan = 0, []
            for kind, dg, m in units:
                plan.append((i if with_max else RING_UNITS // 3 + i, kind, dg, m))
                i += 2 if kind == "neg" else 1
            return plan

        def ring_start(g):
            head = MAXES + 2 + AHEAD
            if isinstance(g, int):
                per = [RING_UNITS - NH] + [RING_UNITS] * (G - 3) + [RING_UNITS - AHEAD] + [NH]
                return head + sum(per[:g])
            return g * RING_UNITS + (head - NH)

        STACKS = 2 * len(Q_PART) + 1

        @block.sync
        def _(sp):
            sp.dma_start(xs[:, 0:NT, :], tiles(x)[:, 0:NT, :]).then_inc(x_in[0], 16)
            def rows(name, src, n, first=False):
                dst, at, done = (vecs, COL[name], vec_in) if first else (vecs2, COL[name] - NV0, vec2_in)
                sp.dma_start(dst[at:at + n, :], src.rearrange("(r p) -> r p", p=P)).then_inc(done, 16)

            rows("norm_w", norm_w, KC, True)
            rows("norm_b", norm_b, KC, True)
            for side, src in enumerate((q_b, k_b)):
                sp.dma_start(vecs[COL["qk_b"]:COL["qk_b"] + HG, side * GC:(side + 1) * GC],
                             src.rearrange("(g c) -> g c", c=GC)).then_inc(vec_in, 16)
            rows("mask0", mask0.rearrange("b t -> (b t)"), B * NT, True)
            for kc in range(KC):
                for side, src in enumerate((q_w, k_w)):
                    sp.dma_start(wqk[:, kc, :, side * GC:(side + 1) * GC],
                                 src[kc * P:(kc + 1) * P, :].rearrange("p (g c) -> p g c", c=GC)).then_inc(w_in, 16)
            sp.dma_start(xs[:, NT:, :], tiles(x)[:, NT:, :]).then_inc(x_in[1], 16)
            sp.dma_start(wv0, v_w.rearrange("(k p) c -> p k c", p=P)).then_inc(wv_in, 16)
            for i, src in enumerate((v_b, out_b, bq, bv, b_out)):
                sp.dma_start(bias_rows[:, i, :], src.partition_broadcast(P)).then_inc(wv_in, 16)
            sp.dma_start(mrow[:, :], mask0.rearrange("b (t p) -> (b t) p", p=P)).then_inc(mask_in, 16)
            for name, src, n in (("sb_w", sb_norm_w, KC), ("sb_b", sb_norm_b, KC),
                                 ("emb_b0", emb_b, 2 * KC), ("ln_w", ln_w, KC), ("ln_b", ln_b, KC), ("bk", bk, KC),
                                 ("ln2_w", ln2_w, KC), ("ln2_b", ln2_b, KC), ("emb_b1", b_emb, 2 * KC),
                                 ("cond", cond.rearrange("b e -> (b e)"), B * EC), ("mask1", mask1.rearrange("b t o -> (b t o)"), B * NT)):
                rows(name, src, n)
            sp.dma_start(wo0[:, :, :], out_w.rearrange("(k p) c -> p k c", p=P)).then_inc(wo_in, 16)
            sp.wait_ge(mparts_ready, 1)
            sp.dma_start(mask_rows.rearrange("r b (t p) -> (b t) r p", p=P), mparts[:, :, :]).then_inc(mask_out, 16)

            def stack(g, slot):
                for side, (dst, order) in enumerate(((qs, Q_PART), (ks, K_PART))):
                    for r, part in enumerate(order):
                        sp.dma_start(dst[r * DH0:(r + 1) * DH0, slot, :, :],
                                     part_rows[g, side * GC:(side + 1) * GC, part, :].rearrange("(j p) n -> p j n", p=DH0)).then_inc(stack_in, 16)
                sp.dma_start(ks[ROW_MASK:ROW_MAX, slot, :, :],
                             mask_rows[:, g // HG, :].unsqueeze(1).to_broadcast([PARTS, GH, T])).then_inc(stack_in, 16)

            def load_max(g, slot):
                sp.wait_ge(cparts_ready, g + 1)
                sp.dma_start(max_rows.rearrange("r j (t p) -> (j t) r p", p=P), cparts[:, :, :]).then_inc(cmax_out, 16)
                sp.wait_ge(cmax_out, (g + 1) * 16)
                sp.dma_start(qs[ROW_MAX:ROWS, slot, :, :], max_rows).then_inc(cmax_in, 16)

            sp.wait_ge(mask_out, 16)
            sp.wait_ge(krows_ready, 1)
            sp.wait_ge(qrows_ready, 1)
            for g in range(HG):
                sp.wait_ge(part3_ready, (g + 1) * NH)
                sp.dma_start(part_rows[g], parts[:, g]).then_inc(parts_out, 16)
                if g < 2:
                    sp.wait_ge(parts_out, 16 * (g + 1))
                    stack(g, g)
                    sp.wait_ge(stack_in, (g + 1) * 16 * STACKS)
            for g in range(HG, G):
                sp.wait_ge(part3_ready, (g + 1) * NH)
                sp.dma_start(part_rows[g], parts[:, g]).then_inc(parts_out, 16)
            sp.wait_ge(parts_out, 16 * G)
            for i, src in enumerate((emb_w, W_emb)):
                sp.dma_start(embw[:, i], src.rearrange("(e p) c -> p e c", p=P)).then_inc(embw_in, 16)
            for i, src in enumerate((Wq, Wk, Wv, W_out)):
                sp.dma_start(w1[:, i], src.rearrange("(k p) c -> p k c", p=P)).then_inc(late_in, 16)
            load_max(0, 0)

            def serve(g, refill):
                if refill:
                    sp.wait_ge(stack_in, (g + 2) * (16 * STACKS))
                    sp.wait_ge(sT_ready, g * UNITS + 4)
                    stack(g + 2, sp.snap((g + 2) % SLOTS))
                load_max(g + 1, sp.snap((g + 1) % SLOTS) if refill else (g + 1) % SLOTS)

            with sp.Fori(0, G - 2) as g:
                serve(g, True)
            sp.wait_ge(sT_ready, (G - 2) * UNITS + 4)
            sp.dma_start(mrows1, mask1.rearrange("b t o -> (b t o)").partition_broadcast(P)).then_inc(mrows_in, 16)
            serve(G - 2, False)
            for b in range(B):
                for half in range(2):
                    sp.wait_ge(pj_read, RING + stage_start("out1", b) + (half + 1) * NT // 4)
                    at = b * NT + half * NT // 2
                    sp.dma_start(tiles(out)[:, at:at + NT // 2, :], xs[:, at:at + NT // 2, :]).then_inc(stored, 16)
            sp.wait_ge(stored, 2 * B * 16)

        @block.gpsimd
        def _(pool):
            pool.memset(ident[:, :], 0.0).then_inc(ident_ready, 1)
            pool.wait_ge(ident_ready, 1)
            pool.affine_select(out=ident[:, :], in_=ident[:, :], compare_op=ALU.not_equal, fill=1.0, base=0,
                               pattern=[[-1, P]], channel_multiplier=1).then_inc(ident_ready, 1)
            pool.wait_ge(ident_ready, 2)
            pool.memset(qs[96:P, :, :, :].rearrange("p s j n -> p (s j n)").bitcast(F32), BF16_ONES).then_inc(qrows_ready, 1)
            pool.memset(ks[96:P, :, :, :].rearrange("p s j n -> p (s j n)").bitcast(F32), BF16_ONES).then_inc(krows_ready, 1)
            pool.wait_ge(krows_ready, 1)
            pool.memset(vs[:, :, :, DH0:32], 1.0).then_inc(ones_ready, 1)
            pool.memset(blocks[:, :], 0.0).then_inc(blocks_ready, 1)
            pool.wait_ge(blocks_ready, 1)
            for j in range(P // DH1):
                pool.wait_ge(blocks_ready, 1 + j)
                pool.memset(blocks[j * DH1:(j + 1) * DH1, j * DH1:(j + 1) * DH1], 1.0).then_inc(blocks_ready, 1)
            pool.wait_ge(blocks_ready, 1 + P // DH1)
            with pool.Fori(0, B) as b:
                for u in range(HG * NH):
                    hg, n = u // NH, u % NH
                    pool.wait_ge(part2_ready, b * (HG * NH) + u + 1)
                    pool.tensor_tensor(parts[:, b * HG + hg, 2, n * HALF:(n + 1) * HALF], rest[:, u % 2, :],
                                       parts[:, b * HG + hg, 1, n * HALF:(n + 1) * HALF], op=ALU.subtract).then_inc(part3_ready, 1)
            pool.wait_ge(wv_in, 16 * 6)
            pool.wait_ge(z_ready, B * NT)
            for b in range(B):
                pool.tensor_tensor(xs[:, b * NT:(b + 1) * NT, :], xs[:, b * NT:(b + 1) * NT, :],
                                   bias_rows[:, 1:2, :].to_broadcast([P, NT, D]), op=ALU.add).then_inc(biased, 1)

            def stage_values(g):
                if not isinstance(g, int):
                    pool.wait_ge(pv_done, g * NT)
                pool.tensor_copy(vs[:, :, :, 0:DH0], v_all[:, g, :, :].rearrange("p t (j c) -> p t j c", j=GH)).then_inc(vs_ready, 1)

            pool.wait_ge(v_ready, B * NT)
            pool.wait_ge(ones_ready, 1)
            stage_values(0)
            with pool.Fori(1, G) as g:
                stage_values(g)
            for b in range(B):
                pool.wait_ge(z_ready, (LN["in1", b] + 1) * NT)
                pool.tensor_tensor(xs[:, b * NT:(b + 1) * NT, :], xs[:, b * NT:(b + 1) * NT, :],
                                   bias_rows[:, 4:5, :].to_broadcast([P, NT, D]), op=ALU.add).then_inc(biased, 1)

        @block.scalar
        def _(act):
            def deviations(kind, b):
                act.wait_ge(var_ready, LN[kind, b] + 1)
                act.activation(std[:, b, :], var[:, b, :], ACT.Sqrt).then_inc(std_ready, 1)

            def scaled(kind, b, A, Bc, func):
                for i in range(TURN):
                    q, kc = i // KC, i % KC
                    act.wait_ge(turn_ready, TURN_NO[kind, b] * TURN + i + 1)
                    act.activation(hT[b][:, kc, q * HALF:(q + 1) * HALF], B8[i], func, scale=A(kc), bias=Bc(kc)).then_inc(turn_read, 1)

            def col(name, i):
                return cols[:, COL[name] + i:COL[name] + i + 1]

            act.wait_ge(cols_ready, 1)
            deviations("in0", 0)
            for b in range(B):
                scaled("in0", b, lambda kc: col("norm_w", kc), lambda kc: col("norm_b", kc), ACT.Identity)
                if b + 1 < B:
                    deviations("in0", b + 1)
                for u in range(HG * NH):
                    hg, n = u // NH, u % NH
                    dst = parts[:, b * HG + hg, :, n * HALF:(n + 1) * HALF]
                    act.wait_ge(pj_ready, b * UNITS_A + u + 1)
                    act.activation(dst[:, 0, :], B8[4 + u % 4], ACT.Identity, bias=col("qk_b", hg)).then_inc(part1_ready, 1)
                    act.wait_ge(pj_read, RING + b * UNITS_A + u + 1)
                    act.activation(dst[:, 1, :], rest[:, u % 2, :], ACT.Copy).then_inc(part2_ready, 1)
                for i in range(NT):
                    act.wait_ge(pj_read, RING + b * UNITS_A + HG * NH + i // 2 + 1)
                    act.activation(v_all[:, b * HG:(b + 1) * HG, i, :], vtmp[:, i // 2 % 2, i % 2 * D:(i % 2 + 1) * D].rearrange("p (g c) -> p g c", g=HG),
                                   ACT.Copy, scale=col("mask0", b * NT + i)).then_inc(v_ready, 1)
            act.wait_ge(cols_ready, 2)
            act.activation(scond[:, :, :], cols[:, COL["cond"]:COL["cond"] + B * EC], ACT.Silu).then_inc(scond_ready, 1)

            def attend(g, first=False, last_group=False):
                for u in range(UNITS):
                    c, j = u // GH, u % GH
                    act.wait_ge(sT_ready, g * UNITS + u + 1)
                    if j == 0 and c >= 2:
                        act.wait_ge(pv_done, g * NT + c - 1)
                    if j == 0 and c < 2 and not first:
                        act.wait_ge(pv_done, (g - 1) * NT + NT - 1 + c)
                    act.activation(prob[:, c % 2, j, :], sT[u % 2][:, :], ACT.Exp).then_inc(exp_done, 1)
                    if u == GH - 1 and not first:
                        finish(g - 1)
                    if u == 2 * GH and last_group:
                        deviations("mid0", 0)

            def finish(g):
                act.wait_ge(pv_done, (g + 1) * NT)
                act.activation(yT[:, :], acc[:, :], ACT.Copy).then_inc(yT_ready, 1)

            act.wait_ge(part3_ready, G * NH)
            attend(0, True)
            with act.Fori(1, G - 1) as g:
                attend(g)
            attend(G - 1, last_group=True)
            finish(G - 1)

            act.wait_ge(mod_ready, 2)
            for b in range(B):
                if b > 0:
                    deviations("mid0", b)
                scaled("mid0", b, lambda kc: modA[:, 0, kc, b:b + 1], lambda kc: modB[:, 0, kc, b:b + 1], ACT.Silu)
            for b in range(B):
                deviations("in1", b)
            for b in range(B):
                scaled("in1", b, lambda kc: col("ln_w", kc), lambda kc: col("ln_b", kc), ACT.Identity)
            for b in range(B):
                for kc in range(KC):
                    act.wait_ge(kmax_ready, b * KC + kc + 1)
                    act.activation(kE[b][:, kc, :], kE[b][:, kc, :], ACT.Exp, bias=kmax[:, b, kc:kc + 1], accum_out=ksum[:, b, kc:kc + 1]).then_inc(kexp_ready, 1)
            for b in range(B):
                for half in range(2):
                    act.wait_ge(qsub_ready, 2 * b + half + 1)
                    rows = q1[b][:, half * NT // 2:(half + 1) * NT // 2, :]
                    act.activation(rows, rows, ACT.Exp).then_inc(qexp_ready, 1)
                for i in range(TURN):
                    act.wait_ge(turn_ready, TURN_NO["kT", b] * TURN + i + 1)
                    act.activation(kN[b][:, 2 * i:2 * i + 2, :].rearrange("p t d -> p (t d)"), B8[i], ACT.Copy).then_inc(turn_read, 1)
                for i in range(NT):
                    act.wait_ge(pj_read, RING + stage_start("values", b) + i // 2 + 1)
                    act.activation(v1[b][:, i, :], v1[b][:, i, :], ACT.Copy, scale=col("mask1", b * NT + i)).then_inc(v1_ready, 1)
                for i in range(TURN):
                    n, kc = i // KC, i % KC
                    act.wait_ge(turn_ready, TURN_NO["qT", b] * TURN + i + 1)
                    act.activation(qT[b][:, kc, n * HALF:(n + 1) * HALF], B8[i], ACT.Copy).then_inc(turn_read, 1)
            for b in range(B):
                deviations("mid1", b)
            for b in range(B):
                scaled("mid1", b, lambda kc: modA[:, 1, kc, b:b + 1], lambda kc: modB[:, 1, kc, b:b + 1], ACT.Silu)

        @block.tensor
        def _(pe):
            def turn_bank(kind, b, i):
                k = TURN_NO[kind, b]
                if k > 0:
                    pe.wait_ge(turn_read, (k - 1) * TURN + i + 1)
                return B8[i]

            def ln_transposes(kind, b, z):
                for i in range(TURN):
                    q, kc = i // KC, i % KC
                    o = turn_bank(kind, b, i)
                    if kc == 0:
                        pe.wait_ge(z_ready, LN[kind, b] * NT + 4 * q + 4)
                    for t in range(4):
                        last = pe.transpose(o[:, t * P:(t + 1) * P], z[:, 4 * q + t, kc * P:(kc + 1) * P], ident[:, :])
                    last.then_inc(turn_ready, 1)
                pe.wait_ge(turn_read, (TURN_NO[kind, b] + 1) * TURN)

            def product(unit, pieces):
                pe.wait_ge(pj_read, unit + 1)
                for terms in pieces:
                    for i, (o, l, r) in enumerate(terms):
                        last = pe.matmul(o, l, r, start=(i == 0), stop=(i == len(terms) - 1))
                last.then_inc(pj_ready, 1)

            def rows_times(b, w, s, o):
                return [[(o[:, i * D:(i + 1) * D], hT[b][:, kc, (2 * s + i) * P:(2 * s + i + 1) * P], w[:, kc, :]) for kc in range(KC)]
                        for i in range(2)]

            def fill(kind, g, m, slot, at, i, banks=sN):
                o = banks[i % len(banks)]
                if kind == "neg" and m == 1:
                    return
                if not isinstance(at, int) or at + i >= len(banks):
                    pe.wait_ge(sN_read, at + i + 1 - len(banks))
                if kind == "max":
                    r, n = m // NH, m % NH
                    j, qt = r // NT, r % NT
                    pe.matmul(o, qs[0:ROW_MAX, slot, j, qt * P:(qt + 1) * P], ks[0:ROW_MAX, slot, j, n * HALF:(n + 1) * HALF],
                              start=True, stop=True).then_inc(sN_ready, 1)
                elif kind == "y":
                    pe.wait_ge(yT_ready, g + 1)
                    for t in range(4):
                        last = pe.transpose(o[:, t * P:(t + 1) * P], yT[:, (4 * m + t) * P:(4 * m + t + 1) * P], ident[:, :])
                    last.then_inc(sN_ready, 1)
                else:
                    pe.wait_ge(neg_ready, g + 1)
                    pe.transpose(o[0:UNITS, 0:P], negmax[:, :], ident[:, :]).then_inc(sN_ready, 2)

            def values(g, c, n):
                if n == 0:
                    pe.wait_ge(exp_done, g * UNITS + (c + 1) * GH)
                    if c == 0:
                        pe.wait_ge(vs_ready, g + 1)
                        if not isinstance(g, int) or g > 0:
                            pe.wait_ge(yT_ready, g)
                for j in range(GH):
                    last = pe.matmul(acc[32 * j:32 * j + 32, n * HALF:(n + 1) * HALF], vs[:, c, j, :], prob[:, c % 2, j, n * HALF:(n + 1) * HALF],
                                     start=(c == 0), stop=(c == NT - 1), skip_group_check=True)
                if n == NH - 1:
                    last.then_inc(pv_done, 1)

            def condition(k):
                if k == 0:
                    pe.wait_ge(sN_read, ring_start(G - 1) + NH)
                    pe.wait_ge(embw_in, 16 * 2)
                    pe.wait_ge(scond_ready, 1)
                l, oc = k // (2 * KC), k % (2 * KC)
                for e in range(EC):
                    last = pe.matmul(sN[0][:, k * B:(k + 1) * B], embw[:, l, e, oc * P:(oc + 1) * P], scond[:, :, e], start=(e == 0), stop=(e == EC - 1))
                if k == 2 * 2 * KC - 1:
                    last.then_inc(emb_ready, 1)

            def attend(g, slots, first=False, last_group=False, more=True):
                at = ring_start(g)
                plan = ring_plan(not first, not last_group, more)
                pe.wait_ge(cmax_in, (g + 1) * 16)
                if not last_group:
                    pe.wait_ge(stack_in, (g + 2) * (16 * STACKS))
                turn = done = 0

                def turns(k):
                    nonlocal turn, done
                    turn += k
                    while done < len(plan) and plan[done][0] * TURNS < turn * RING_UNITS:
                        i, kind, dg, m = plan[done]
                        if kind == "max" and dg == 2 and m == 0:
                            pe.wait_ge(stack_in, (g + 3) * (16 * STACKS))
                        fill(kind, g + dg, m, slots[max(dg, 0)], at, m if last_group else i)
                        done += 1

                for c in range(NT):
                    for j in range(GH):
                        u = c * GH + j
                        if u >= 2 or not first:
                            pe.wait_ge(exp_done, g * UNITS + u - 1)
                        for n in range(NH):
                            last = pe.matmul(sT[u % 2][:, n * HALF:(n + 1) * HALF], ks[0:ROWS, slots[0], j, c * P:(c + 1) * P],
                                             qs[0:ROWS, slots[0], j, n * HALF:(n + 1) * HALF], start=True, stop=True)
                            if n == NH - 1:
                                last.then_inc(sT_ready, 1)
                            turns(1)
                        if c > 0 and j % 2 == 1:
                            turns(VALUES_TURNS // 2)
                            values(g, c - 1, j // 2)
                            turns(VALUES_TURNS // 2)
                        if c == 0 and not first and 1 <= j <= NH:
                            turns(VALUES_TURNS // 2)
                            values(g - 1, NT - 1, j - 1)
                            turns(VALUES_TURNS // 2)
                        if last_group and u >= UNITS // 2 and u % 2 == 1:
                            condition(u // 2 - UNITS // 4)
                assert first or turn == TURNS
                turns(TURNS)
                assert done == len(plan)

            pe.wait_ge(vec_in, 16 * 5)
            pe.wait_ge(ident_ready, 2)
            pe.transpose(B8[7][:, 0:NV0], vecs[:, :], ident[0:NV0, 0:NV0]).then_inc(vecT_ready, 1)
            pe.wait_ge(cols_ready, 1)
            for b in range(B):
                ln_transposes("in0", b, zs_in[b])
                if b == 0:
                    pe.wait_ge(w_in, 16 * 2 * KC)
                for u in range(UNITS_A):
                    hg, n, s = u // NH, u % NH, u - HG * NH
                    if b == 0 and s == 0:
                        pe.wait_ge(wv_in, 16 * 6)
                    if s < 0:
                        product(b * UNITS_A + u, [[(B8[4 + u % 4], wqk[:, kc, hg, :], hT[b][:, kc, n * HALF:(n + 1) * HALF]) for kc in range(KC)]])
                    else:
                        product(b * UNITS_A + u, rows_times(b, wv0, s, B8[4 + u % 4]))
                    if b == B - 1:
                        if u == 0:
                            pe.wait_ge(stack_in, 16 * STACKS)
                        for i, kind, g, m in prologue_share(u):
                            fill(kind, g, m, g, 0, i, B8[0:4])
                if b == 0:
                    pe.wait_ge(vec2_in, 16 * 11)
                    pe.transpose(B8[0][:, NV0:NV], vecs2[:, :], ident[0:NV - NV0, 0:NV - NV0]).then_inc(vecT_ready, 1)
                    pe.wait_ge(cols_ready, 2)

            for i, kind, g, m in prologue_rest():
                if (kind, g, m) == ("max", 1, 0):
                    pe.wait_ge(stack_in, 2 * 16 * STACKS)
                fill(kind, g, m, g, 0, i, B8[0:4])
            pe.wait_ge(pj_read, RING + B * UNITS_A)
            pe.wait_ge(sN_read, len(prologue))
            attend(0, (0, 1, 2), first=True)
            with pe.Fori(1, G - 2) as g:
                attend(g, (pe.snap(g % SLOTS), pe.snap((g + 1) % SLOTS), pe.snap((g + 2) % SLOTS)))
            attend(G - 2, ((G - 2) % SLOTS, (G - 1) % SLOTS, 0), more=False)
            attend(G - 1, ((G - 1) % SLOTS, 0, 0), last_group=True)
            for n in range(NH):
                values(G - 1, NT - 1, n)
            pe.wait_ge(exp_done, G * UNITS)
            pe.wait_ge(mod_step, 2)
            for m in range(NH):
                fill("y", G - 1, m, 0, ring_start(G), m)
            pe.wait_ge(wo_in, 16)
            pe.wait_ge(late_in, 16 * 4)
            pe.wait_ge(sN_read, ring_start(G) + NH)

            def ring(at, i):
                return B8[4 + (at + i) % RING]

            def stage(name, b, w):
                at = stage_start(name, b)
                for s in range(NT // 2):
                    product(at + s, rows_times(b, w, s, ring(at, s)))

            for b in range(B):
                ln_transposes("mid0", b, zs[b])
                stage("out0", b, wo0)
            for b in range(B):
                ln_transposes("in1", b, zs[b])
                at = stage_start("keys", b)
                for u in range(KC * NH):
                    kc, n = u // NH, u % NH
                    product(at + u, [[(ring(at, u), w1[:, 1, i, kc * P:(kc + 1) * P], hT[b][:, i, n * HALF:(n + 1) * HALF]) for i in range(KC)]])
            for b in range(B):
                stage("queries", b, w1[:, 0])
            for b in range(B):
                for i in range(TURN):
                    o = turn_bank("kT", b, i)
                    if i == 0:
                        pe.wait_ge(kexp_ready, (b + 1) * KC)
                    for t in range(2):
                        for kc in range(KC):
                            last = pe.transpose(o[:, (t * KC + kc) * P:(t * KC + kc + 1) * P],
                                                kE[b][:, kc, (2 * i + t) * P:(2 * i + t + 1) * P], ident[:, :])
                    last.then_inc(turn_ready, 1)
                stage("values", b, w1[:, 2])
                for i in range(TURN):
                    n, kc = i // KC, i % KC
                    o = turn_bank("qT", b, i)
                    pe.wait_ge(qexp_ready, 2 * b + n + 1)
                    for t in range(4):
                        last = pe.transpose(o[:, t * P:(t + 1) * P], q1[b][:, 4 * n + t, kc * P:(kc + 1) * P], ident[:, :])
                    last.then_inc(turn_ready, 1)
            for b in range(B):
                pe.wait_ge(turn_read, (TURN_NO["kT", b] + 1) * TURN)
                pe.wait_ge(v1_ready, (b + 1) * NT)
                at = stage_start("att", b)
                for kc in range(KC):
                    product(at + kc, [[(ring(at, kc)[:, 0:P], kN[b][:, t, kc * P:(kc + 1) * P], v1[b][:, t, kc * P:(kc + 1) * P]) for t in range(NT)]])
            for b in range(B):
                pe.wait_ge(turn_read, (TURN_NO["qT", b] + 1) * TURN)
                pe.wait_ge(pj_read, RING + stage_start("att", b) + KC)
                at = stage_start("y", b)
                for s in range(NT // 2):
                    product(at + s, [[(ring(at, s)[:, i * D + kc * P:i * D + (kc + 1) * P], qT[b][:, kc, (2 * s + i) * P:(2 * s + i + 1) * P], att[:, b, kc, :])]
                                     for i in range(2) for kc in range(KC)])
            for b in range(B):
                ln_transposes("mid1", b, zs[b])
                stage("out1", b, w1[:, 3])

        @block.vector
        def _(dve):
            def layer_norm(kind, b, src, z):
                L = LN[kind, b]
                base = L * LN_STEPS
                for t in range(NT):
                    dve.bn_stats(stats[:, b, t, :], src(t)).then_inc(ln_step, 1)
                dve.wait_ge(ln_step, base + NT)
                for t in range(NT):
                    dve.bn_aggr(mv[:, b, t, :], stats[:, b, t, :]).then_inc(ln_step, 1)
                dve.wait_ge(ln_step, base + 2 * NT)
                dve.tensor_scalar_add(var[:, b, :], mv[:, b, :, 1], EPS).then_inc(var_ready, 1)
                dve.wait_ge(std_ready, L + 1)
                dve.reciprocal(rstd[:, b, :], std[:, b, :]).then_inc(ln_step, 1)
                dve.wait_ge(ln_step, base + LN_STEPS)
                for t in range(NT):
                    dst = z[:, t, :]
                    s = src(t)
                    if len(s.shape) == 3:
                        dst = dst.rearrange("p (g c) -> p g c", g=HG)
                    dve.tensor_scalar(dst, s, mv[:, b, t, 0:1], rstd[:, b, t:t + 1], op0=ALU.subtract, op1=ALU.mult).then_inc(z_ready, 1)

            dve.memset(negmax[:, 0:1], 0.0).then_inc(pj_read, RING)
            dve.wait_ge(vecT_ready, 1)
            dve.tensor_copy(cols[:, 0:NV0], B8[7][:, 0:NV0]).then_inc(cols_ready, 1)
            def read(kind, g, m, at, i, banks=sN):
                src = banks[i % len(banks)]
                if kind == "neg" and m == 1:
                    return
                if kind == "neg":
                    dve.wait_ge(sN_ready, at + i + 2)
                    if not isinstance(g, int) or g > 0:
                        dve.wait_ge(cmax_out, g * 16)
                    src, base = src[0:UNITS, 0:P], g * 2
                    dve.tensor_copy(cparts[:, 0, :], src).then_inc(csplit_step, 1)
                    dve.wait_ge(csplit_step, base + 1)
                    dve.tensor_tensor(crest[:, 0, :], src, cparts[:, 0, :], op=ALU.subtract).then_inc(sN_read, 2)
                    dve.wait_ge(sN_read, at + i + 2)
                    dve.tensor_copy(cparts[:, 1, :], crest[:, 0, :]).then_inc(csplit_step, 1)
                    dve.wait_ge(csplit_step, base + 2)
                    dve.tensor_tensor(cparts[:, 2, :], crest[:, 0, :], cparts[:, 1, :], op=ALU.subtract).then_inc(cparts_ready, 1)
                    return
                dve.wait_ge(sN_ready, at + i + 1)
                if kind == "max":
                    r, n = m // NH, m % NH
                    dve.tensor_reduce(halfmax[:, r, n:n + 1], src, axis=AX.X, op=ALU.max, negate=True).then_inc(sN_read, 1)
                    if m == MAXES - 1:
                        dve.wait_ge(sN_read, at + i + 1)
                        dve.tensor_reduce(negmax[:, :], halfmax[:, :, :], axis=AX.X, op=ALU.min).then_inc(neg_ready, 1)
                        dve.wait_ge(neg_ready, g + 1)
                else:
                    src = src.rearrange("p (u c) -> p u c", c=32)
                    dve.reciprocal(rden[:, m, :, :], src[:, :, DH0:DH0 + 1]).then_inc(rden_ready, 1)
                    dve.wait_ge(rden_ready, g * NH + m + 1)
                    dve.tensor_tensor(y_all[:, g, 4 * m:4 * m + 4, :].rearrange("p t (j c) -> p (t j) c", c=DH0), src[:, :, 0:DH0],
                                      rden[:, m, :, :].to_broadcast([P, 4 * GH, DH0]), op=ALU.mult).then_inc(sN_read, 1)

            for b in range(B):
                dve.wait_ge(x_in[b], 16)
                layer_norm("in0", b, lambda t: xs[:, b * NT + t, :], zs_in[b])
            dve.wait_ge(mask_in, 16)
            dve.tensor_scalar(mrest[:, 0, :], mrow[:, :], 1.0, BIG, op0=ALU.subtract, op1=ALU.mult).then_inc(msplit_step, 1)
            dve.wait_ge(msplit_step, 1)
            dve.tensor_copy(mparts[:, 0, :], mrest[:, 0, :]).then_inc(msplit_step, 1)
            dve.wait_ge(msplit_step, 2)
            dve.tensor_tensor(mrest[:, 1, :], mrest[:, 0, :], mparts[:, 0, :], op=ALU.subtract).then_inc(msplit_step, 1)
            dve.wait_ge(msplit_step, 3)
            dve.tensor_copy(mparts[:, 1, :], mrest[:, 1, :]).then_inc(msplit_step, 1)
            dve.wait_ge(msplit_step, 4)
            dve.tensor_tensor(mparts[:, 2, :], mrest[:, 1, :], mparts[:, 1, :], op=ALU.subtract).then_inc(mparts_ready, 1)
            for b in range(B):
                def share(u):
                    if b == B - 1:
                        for i, kind, g, m in prologue_share(u):
                            read(kind, g, m, 0, i, B8[0:4])

                for u in range(HG * NH):
                    hg, n = u // NH, u % NH
                    c = COL["qk_b"] + hg
                    dve.wait_ge(part1_ready, b * (HG * NH) + u + 1)
                    if b > 0 or u >= 2:
                        dve.wait_ge(part3_ready, b * (HG * NH) + u - 1)
                    dve.scalar_tensor_tensor(out=rest[:, u % 2, :], in0=B8[4 + u % 4], scalar=cols[:, c:c + 1],
                                             in1=parts[:, b * HG + hg, 0, n * HALF:(n + 1) * HALF],
                                             op0=ALU.add, op1=ALU.subtract).then_inc(pj_read, 1)
                    share(u)
                if b == 0:
                    dve.wait_ge(wv_in, 16 * 6)
                for s in range(NT // 2):
                    u = HG * NH + s
                    dve.wait_ge(pj_ready, b * UNITS_A + u + 1)
                    if b > 0 or s >= 2:
                        dve.wait_ge(v_ready, b * NT + 2 * (s - 1))
                    dve.tensor_tensor(vtmp[:, s % 2, :].rearrange("p (t d) -> p t d", d=D), B8[4 + u % 4].rearrange("p (t d) -> p t d", d=D),
                                      bias_rows[:, 0:1, :].to_broadcast([P, 2, D]), op=ALU.add).then_inc(pj_read, 1)
                    share(u)
                if b == 0:
                    dve.wait_ge(vecT_ready, 2)
                    dve.tensor_copy(cols[:, NV0:NV], B8[0][:, NV0:NV]).then_inc(cols_ready, 1)
            def beside(g, first=False, last_group=False, more=True):
                for i, kind, dg, m in ring_plan(not first, not last_group, more):
                    read(kind, g + dg, m, ring_start(g), i if not last_group else m)

            for i, kind, g, m in prologue_rest():
                read(kind, g, m, 0, i, B8[0:4])
            beside(0, first=True)
            with dve.Fori(1, G - 2) as g:
                beside(g)
            beside(G - 2, more=False)
            layer_norm("mid0", 0, lambda t: y_all[:, 0:HG, t, :], zs[0])
            beside(G - 1, last_group=True)
            dve.wait_ge(mrows_in, 16)
            dve.tensor_scalar(mrows1, mrows1, 1.0, BIG, op0=ALU.subtract, op1=ALU.mult).then_inc(mrows_ready, 1)
            def by_col(name, n):
                return cols[:, COL[name]:COL[name] + n].unsqueeze(2).to_broadcast([P, n, B])

            dve.wait_ge(emb_ready, 1)
            bank_emb = sN[0][:, 0:2 * 2 * KC * B].rearrange("p (l o b) -> p l o b", l=2, b=B)
            for l in range(2):
                dve.tensor_tensor(emb[:, l], bank_emb[:, l], by_col(f"emb_b{l}", 2 * KC), op=ALU.add).then_inc(mod_step, 1)
            dve.wait_ge(mod_step, 2)
            for l, (w, b) in enumerate((("sb_w", "sb_b"), ("ln2_w", "ln2_b"))):
                for mod, name in ((modA, w), (modB, b)):
                    dve.scalar_tensor_tensor(out=mod[:, l], in0=emb[:, l, 0:KC, :], scalar=1.0, in1=by_col(name, KC), op0=ALU.add, op1=ALU.mult).then_inc(mod_step, 1)
            dve.wait_ge(mod_step, 6)
            for l in range(2):
                dve.tensor_tensor(modB[:, l], modB[:, l], emb[:, l, KC:2 * KC, :], op=ALU.add).then_inc(mod_ready, 1)
            for m in range(NH):
                read("y", G - 1, m, ring_start(G), m)
            dve.wait_ge(sN_read, ring_start(G) + NH)

            def ring(at, i):
                return B8[4 + (at + i) % RING]

            def pair(o):
                return o.rearrange("p (t d) -> p t d", d=D)

            def add_rows(name, b):
                at = stage_start(name, b)
                for s in range(NT // 2):
                    xt = xs[:, b * NT + 2 * s:b * NT + 2 * s + 2, :]
                    dve.wait_ge(pj_ready, at + s + 1)
                    dve.tensor_tensor(xt, xt, pair(ring(at, s)), op=ALU.add).then_inc(pj_read, 1)

            def add_bias(name, b, dst, row):
                at = stage_start(name, b)
                for s in range(NT // 2):
                    dve.wait_ge(pj_ready, at + s + 1)
                    dve.tensor_tensor(dst[:, 2 * s:2 * s + 2, :], pair(ring(at, s)), bias_rows[:, row:row + 1, :].to_broadcast([P, 2, D]),
                                      op=ALU.add).then_inc(pj_read, 1)

            def by_head(b, small, half):
                t0, t1 = half * NT // 2, (half + 1) * NT // 2
                return (q1[b][:, t0:t1, :].rearrange("p t (h c) -> p (t h) c", c=DH1), small[:, b, t0:t1].rearrange("p t h o -> p (t h) o"))

            dve.wait_ge(biased, B)
            for b in range(B):
                if b > 0:
                    layer_norm("mid0", b, lambda t: y_all[:, b * HG:(b + 1) * HG, t, :], zs[b])
            for b in range(B):
                add_rows("out0", b)
            for b in range(B):
                dve.wait_ge(pj_read, RING + stage_start("out0", b) + NT // 2)
                layer_norm("in1", b, lambda t: xs[:, b * NT + t, :], zs[b])
            dve.wait_ge(mrows_ready, 1)
            for b in range(B):
                at = stage_start("keys", b)
                for u in range(KC * NH):
                    kc, n = u // NH, u % NH
                    c = COL["bk"] + kc
                    dve.wait_ge(pj_ready, at + u + 1)
                    dve.scalar_tensor_tensor(out=kE[b][:, kc, n * HALF:(n + 1) * HALF], in0=ring(at, u), scalar=cols[:, c:c + 1],
                                             in1=mrows1[:, b * T + n * HALF:b * T + (n + 1) * HALF], op0=ALU.add, op1=ALU.add).then_inc(pj_read, 1)
                    if n == NH - 1:
                        dve.wait_ge(pj_read, RING + at + u + 1)
                        dve.tensor_reduce(kmax[:, b, kc:kc + 1], kE[b][:, kc, :], axis=AX.X, op=ALU.max, negate=True).then_inc(kmax_ready, 1)
            for b in range(B):
                add_bias("queries", b, q1[b], 2)
                dve.wait_ge(pj_read, RING + stage_start("queries", b) + NT // 2)
                for half in range(2):
                    rows, mx = by_head(b, qmax, half)
                    dve.tensor_reduce(mx, rows, axis=AX.X, op=ALU.max).then_inc(q_step, 1)
                    dve.wait_ge(q_step, b * 2 + half + 1)
                    dve.tensor_tensor(rows, rows, mx.to_broadcast([P, NT // 2 * H1, DH1]), op=ALU.subtract).then_inc(qsub_ready, 1)
            for b in range(B):
                add_bias("values", b, v1[b], 3)
                for half in range(2):
                    rows, sums = by_head(b, qsum, half)
                    dve.wait_ge(qexp_ready, 2 * b + half + 1)
                    dve.tensor_reduce(sums, rows, axis=AX.X, op=ALU.add).then_inc(q_step, 1)
                dve.wait_ge(q_step, 2 * B + 2 * b + 2)
                dve.reciprocal(rqsum[:, b], qsum[:, b]).then_inc(rq_ready, 1)
                dve.wait_ge(kexp_ready, (b + 1) * KC)
                dve.reciprocal(rksum[:, b, :], ksum[:, b, :]).then_inc(rk_ready, 1)
            for b in range(B):
                dve.wait_ge(rk_ready, b + 1)
                at = stage_start("att", b)
                for kc in range(KC):
                    dve.wait_ge(pj_ready, at + kc + 1)
                    dve.scalar_tensor_tensor(out=att[:, b, kc, :], in0=ring(at, kc)[:, 0:P], scalar=rksum[:, b, kc:kc + 1], in1=blocks[:, :],
                                             op0=ALU.mult, op1=ALU.mult).then_inc(pj_read, 1)
            for b in range(B):
                dve.wait_ge(rq_ready, b + 1)
                at = stage_start("y", b)
                for s in range(NT // 2):
                    dve.wait_ge(pj_ready, at + s + 1)
                    dve.tensor_tensor(q1[b][:, 2 * s:2 * s + 2, :].rearrange("p t (h c) -> p (t h) c", c=DH1), ring(at, s).rearrange("p (h c) -> p h c", c=DH1),
                                      rqsum[:, b, 2 * s:2 * s + 2].rearrange("p t h o -> p (t h) o").to_broadcast([P, 2 * H1, DH1]), op=ALU.mult).then_inc(pj_read, 1)
            for b in range(B):
                dve.wait_ge(pj_read, RING + stage_start("y", b) + NT // 2)
                layer_norm("mid1", b, lambda t: q1[b][:, t, :], zs[b])
            for b in range(B):
                dve.wait_ge(biased, B + b + 1)
                add_rows("out1", b)


_INS = ["x", "cond_2048", "mask_BxS_ff1", "mask_BxSx1_fk1",
        "L0_cond_norm_w", "L0_cond_norm_b", "L0_cond_q_w", "L0_cond_q_b", "L0_cond_k_w", "L0_cond_k_b", "L0_cond_v_w", "L0_cond_v_b",
        "L0_cond_emb_w", "L0_cond_emb_b", "L0_cond_sb_norm_w", "L0_cond_sb_norm_b", "L0_cond_out_w", "L0_cond_out_b",
        "L1_cond_ln_w", "L1_cond_ln_b", "L1_cond_Wq", "L1_cond_bq", "L1_cond_Wk", "L1_cond_bk", "L1_cond_Wv", "L1_cond_bv",
        "L1_cond_W_emb", "L1_cond_b_emb", "L1_cond_ln2_w", "L1_cond_ln2_b", "L1_cond_W_out", "L1_cond_b_out"]


def kernel(**inputs):
    import concourse.bacc as bacc
    from concourse.bass_utils import run_bass_kernel_spmd

    nc = bacc.Bacc("TRN2", target_bir_lowering=False, num_devices=1)
    arrays, args = {}, []
    for name in _INS:
        a = np.ascontiguousarray(inputs[name])
        arrays[f"in_{name}"] = a
        args.append(nc.dram_tensor(f"in_{name}", a.shape, mybir.dt.from_np(a.dtype), kind="ExternalInput").ap())
    shape = arrays["in_x"].shape
    args.append(nc.dram_tensor("out_x", shape, mybir.dt.float32, kind="ExternalOutput").ap())
    two_layer_conditioned_attention(nc, *args)
    r = run_bass_kernel_spmd(nc, [arrays], core_ids=[0])
    return r.results[0]["out_x"]
```
